# Optimizing a Trainium2 kernel written in Bass

```python
import numpy as np
import jax
import jax.numpy as jnp

def _softmax(x, axis=-1):
    return jax.nn.softmax(x, axis=axis)

def _gelu(x):
    return jax.nn.gelu(x, approximate=True)

def _silu(x):
    return jax.nn.silu(x)

def _sigmoid(x):
    return jax.nn.sigmoid(x)

def _layernorm(x, axis=-1, eps=1e-05):
    m = jnp.mean(x, axis=axis, keepdims=True)
    v = jnp.var(x, axis=axis, keepdims=True)
    return (x - m) / jnp.sqrt(v + eps)

def _scatter_add(tgt, idx, src, axis=0):
    return tgt.at[idx].add(src)

def _segment_sum(src, seg, n):
    return jax.ops.segment_sum(src, seg, n)
kernel_name = 'mk_flamingo_gated_d1_seqx_r4_4de3cc'

def setup_inputs(seed: int=0):
    np.random.seed(seed)
    _w = jnp.asarray

    def _rec_inputs():
        import jax
        import jax.numpy as jnp
        _rk = jax.random.key(seed)
        x = 7.22e-05 + 1 * jax.random.normal(jax.random.fold_in(_rk, 1), (16, 256, 512), jnp.float32)
        _lenS = 256 - jax.random.randint(jax.random.fold_in(_rk, 7), (16,), 0, max(1, 256 // 4) + 1, jnp.int32)
        _lenS2 = 256 - jax.random.randint(jax.random.fold_in(_rk, 8), (16,), 0, max(1, 256 // 4) + 1, jnp.int32)
        _ctx_2048P = jax.random.normal(jax.random.fold_in(_rk, 11), (16, 16, 512), jnp.float32)
        _ctx_2048c = jax.random.dirichlet(jax.random.fold_in(_rk, 511), 0.3 * jnp.ones((16,), jnp.float32), (16, 256))
        _ctx_2048t = jnp.einsum('bsk,bkd->bsd', _ctx_2048c, _ctx_2048P)
        _ctx_2048t = _ctx_2048t * jax.lax.rsqrt(jnp.mean(jnp.square(_ctx_2048t)) + 1e-12) * 0.953939
        ctx_2048 = 4.13588e-05 + 0.999923 * (_ctx_2048t + 0.3 * jax.random.normal(jax.random.fold_in(_rk, 611), (16, 256, 512), jnp.float32))
        _g = jax.random.normal(jax.random.fold_in(_rk, 9001), (2, 1), jnp.float32)
        _g = jnp.sign(_g) * jnp.maximum(jnp.abs(_g), 1.0) + (_g == 0) * 1.0
        g_xattn = _g[0]
        g_ffn = _g[1]
        return (x, ctx_2048, g_xattn, g_ffn)
    x, ctx_2048, g_xattn, g_ffn = _rec_inputs()

    def _L0_xattn_setup():
        import jax, jax.numpy as jnp
        import numpy as np
        B, S, DIM, HD = (4, 256, 512, 128)
        H = DIM // HD
        GN_EPS = 0.001

        def _decay_masks(n_heads, seq_len):
            gam = 1.0 - 2.0 ** (-5.0 - jnp.arange(n_heads, dtype=jnp.float32))
            idx = jnp.arange(seq_len, dtype=jnp.float32)
            expo = idx[None, :] - idx[:, None]
            D = jnp.where(expo[None, :, :] <= 0, gam[:, None, None] ** expo[None, :, :], 0.0)
            return D / jnp.sqrt(D.sum(axis=-1))[:, None, :]
        key = jax.random.key(seed)
        ks = jax.random.split(key, 8)
        x = jax.random.normal(ks[0], (B, S, DIM), dtype=jnp.float32)
        k = jax.random.normal(ks[1], (B, S, DIM), dtype=jnp.float32)
        v = jax.random.normal(ks[2], (B, S, DIM), dtype=jnp.float32)
        Wh = jax.random.normal(ks[3], (H, HD, HD), dtype=jnp.float32) / np.sqrt(HD)
        wg_w = jax.random.normal(ks[4], (DIM, DIM), dtype=jnp.float32) / np.sqrt(DIM)
        wo_w = jax.random.normal(ks[5], (DIM, DIM), dtype=jnp.float32) / np.sqrt(DIM)
        gn_gamma = jnp.ones((DIM,), dtype=jnp.float32)
        gn_beta = jnp.zeros((DIM,), dtype=jnp.float32)
        return {'x': x, 'k': k, 'v': v, 'Wh': Wh, 'wg_w': wg_w, 'wo_w': wo_w, 'gn_gamma': gn_gamma, 'gn_beta': gn_beta}
    _L0_xattn_all = _L0_xattn_setup()
    _L0_xattn_in = {k: v for k, v in _L0_xattn_all.items() if k in ('Wh', 'wg_w', 'wo_w', 'gn_gamma', 'gn_beta')}
    del _L0_xattn_all

    def _L0_ffn_setup():
        import jax, jax.numpy as jnp
        import numpy as np
        H = 512
        I = 352
        E = 8
        TOP_K = 2
        N_SHARED = 2
        I_SH = I * N_SHARED
        NORM_TOPK = True

        def _moe_forward(hidden_states, gate_w, expert_gate, expert_up, expert_down, shared_gate, shared_up, shared_down):
            bsz, seq_len, hdim = hidden_states.shape
            x = hidden_states.reshape(-1, hdim)
            logits = x @ gate_w.T
            probs = jax.nn.softmax(logits, axis=-1)
            routing_weights, selected = jax.lax.top_k(probs, TOP_K)
            if NORM_TOPK:
                routing_weights = routing_weights / (routing_weights.sum(axis=-1, keepdims=True) + 1e-20)
            combine = jnp.sum(jax.nn.one_hot(selected, E, dtype=routing_weights.dtype) * routing_weights[..., None], axis=1)
            g_sh = x @ shared_gate.T
            u_sh = x @ shared_up.T
            out = jax.nn.silu(g_sh) * u_sh @ shared_down.T
            g = jnp.einsum('nh,eih->nei', x, expert_gate)
            u = jnp.einsum('nh,eih->nei', x, expert_up)
            y = jnp.einsum('nei,ehi->neh', jax.nn.silu(g) * u, expert_down)
            out = out + jnp.einsum('neh,ne->nh', y, combine)
            return out.reshape(bsz, seq_len, hdim)
        key = jax.random.key(seed)
        ks = jax.random.split(key, 8)
        s = 0.02
        return {'hidden_states': jax.random.normal(ks[0], (1, 256, H), dtype=jnp.float32), 'gate_w': jax.random.normal(ks[1], (E, H), dtype=jnp.float32) * s, 'expert_gate': jax.random.normal(ks[2], (E, I, H), dtype=jnp.float32) * s, 'expert_up': jax.random.normal(ks[3], (E, I, H), dtype=jnp.float32) * s, 'expert_down': jax.random.normal(ks[4], (E, H, I), dtype=jnp.float32) * s, 'shared_gate': jax.random.normal(ks[5], (I_SH, H), dtype=jnp.float32) * s, 'shared_up': jax.random.normal(ks[6], (I_SH, H), dtype=jnp.float32) * s, 'shared_down': jax.random.normal(ks[7], (H, I_SH), dtype=jnp.float32) * s}
    _L0_ffn_all = _L0_ffn_setup()
    _L0_ffn_in = {k: v for k, v in _L0_ffn_all.items() if k in ('gate_w', 'expert_gate', 'expert_up', 'expert_down', 'shared_gate', 'shared_up', 'shared_down')}
    del _L0_ffn_all
    return {'x': x, 'ctx_2048': ctx_2048, 'g_xattn': g_xattn, 'g_ffn': g_ffn, 'L0_xattn_Wh': _L0_xattn_in['Wh'], 'L0_xattn_wg_w': _L0_xattn_in['wg_w'], 'L0_xattn_wo_w': _L0_xattn_in['wo_w'], 'L0_xattn_gn_gamma': _L0_xattn_in['gn_gamma'], 'L0_xattn_gn_beta': _L0_xattn_in['gn_beta'], 'L0_ffn_gate_w': _L0_ffn_in['gate_w'], 'L0_ffn_expert_gate': _L0_ffn_in['expert_gate'], 'L0_ffn_expert_up': _L0_ffn_in['expert_up'], 'L0_ffn_expert_down': _L0_ffn_in['expert_down'], 'L0_ffn_shared_gate': _L0_ffn_in['shared_gate'], 'L0_ffn_shared_up': _L0_ffn_in['shared_up'], 'L0_ffn_shared_down': _L0_ffn_in['shared_down']}

def reference(x, ctx_2048, g_xattn, g_ffn, L0_xattn_Wh, L0_xattn_wg_w, L0_xattn_wo_w, L0_xattn_gn_gamma, L0_xattn_gn_beta, L0_ffn_gate_w, L0_ffn_expert_gate, L0_ffn_expert_up, L0_ffn_expert_down, L0_ffn_shared_gate, L0_ffn_shared_up, L0_ffn_shared_down):
    import jax
    import jax.numpy as jnp

    def _L0_xattn_ref(x, k, v, Wh, wg_w, wo_w, gn_gamma, gn_beta):
        import jax, jax.numpy as jnp
        import numpy as np
        B, S, DIM, HD = (4, 256, 512, 128)
        H = DIM // HD
        GN_EPS = 0.001

        def _decay_masks(n_heads, seq_len):
            gam = 1.0 - 2.0 ** (-5.0 - jnp.arange(n_heads, dtype=jnp.float32))
            idx = jnp.arange(seq_len, dtype=jnp.float32)
            expo = idx[None, :] - idx[:, None]
            D = jnp.where(expo[None, :, :] <= 0, gam[:, None, None] ** expo[None, :, :], 0.0)
            return D / jnp.sqrt(D.sum(axis=-1))[:, None, :]
        b, s, dim = x.shape
        h, hd, _ = Wh.shape
        xh = x.reshape(b, s, h, hd)
        kh = k.reshape(b, s, h, hd)
        vh = v.reshape(b, s, h, hd)
        Q = jnp.einsum('bshd,hde->bshe', xh, Wh)
        K = jnp.einsum('bshd,hde->bshe', kh, Wh)
        V = jnp.einsum('bshd,hde->bshe', vh, Wh)
        scores = jnp.einsum('bshe,bthe->bhst', Q, K) / jnp.sqrt(jnp.float32(hd))
        Dn = _decay_masks(h, s)
        masked = scores * Dn[None, :, :, :]
        A = jnp.maximum(jnp.abs(masked.sum(axis=0)), 1.0)
        O = jnp.einsum('hst,bthe->bshe', A, V).reshape(b, s, dim)
        mu = O.mean(axis=-1, keepdims=True)
        var = O.var(axis=-1, keepdims=True)
        Y = (O - mu) / jnp.sqrt(var + GN_EPS) * gn_gamma + gn_beta
        W = jax.nn.relu(x @ wg_w)
        return W * Y @ wo_w

    def _L0_ffn_ref(hidden_states, gate_w, expert_gate, expert_up, expert_down, shared_gate, shared_up, shared_down):
        import jax, jax.numpy as jnp
        import numpy as np
        H = 512
        I = 352
        E = 8
        TOP_K = 2
        N_SHARED = 2
        I_SH = I * N_SHARED
        NORM_TOPK = True

        def _moe_forward(hidden_states, gate_w, expert_gate, expert_up, expert_down, shared_gate, shared_up, shared_down):
            bsz, seq_len, hdim = hidden_states.shape
            x = hidden_states.reshape(-1, hdim)
            logits = x @ gate_w.T
            probs = jax.nn.softmax(logits, axis=-1)
            routing_weights, selected = jax.lax.top_k(probs, TOP_K)
            if NORM_TOPK:
                routing_weights = routing_weights / (routing_weights.sum(axis=-1, keepdims=True) + 1e-20)
            combine = jnp.sum(jax.nn.one_hot(selected, E, dtype=routing_weights.dtype) * routing_weights[..., None], axis=1)
            g_sh = x @ shared_gate.T
            u_sh = x @ shared_up.T
            out = jax.nn.silu(g_sh) * u_sh @ shared_down.T
            g = jnp.einsum('nh,eih->nei', x, expert_gate)
            u = jnp.einsum('nh,eih->nei', x, expert_up)
            y = jnp.einsum('nei,ehi->neh', jax.nn.silu(g) * u, expert_down)
            out = out + jnp.einsum('neh,ne->nh', y, combine)
            return out.reshape(bsz, seq_len, hdim)
        return _moe_forward(hidden_states, gate_w, expert_gate, expert_up, expert_down, shared_gate, shared_up, shared_down)
    x = x + jnp.tanh(g_xattn[0]) * _L0_xattn_ref(_layernorm(x, axis=-1), ctx_2048, ctx_2048, L0_xattn_Wh, L0_xattn_wg_w, L0_xattn_wo_w, L0_xattn_gn_gamma, L0_xattn_gn_beta)
    x = x + jnp.tanh(g_ffn[0]) * _L0_ffn_ref(_layernorm(x, axis=-1), L0_ffn_gate_w, L0_ffn_expert_gate, L0_ffn_expert_up, L0_ffn_expert_down, L0_ffn_shared_gate, L0_ffn_shared_up, L0_ffn_shared_down)
    return x

_drawn_inputs = setup_inputs


def setup_inputs(seed=0):
    import zlib

    import numpy as np

    out = dict(_drawn_inputs(seed))
    spreads = {'L0_xattn_gn_gamma': (1.0, 0.2), 'L0_xattn_gn_beta': (0.0, 0.1)}
    factors = {'L0_ffn_gate_w': 2.721}
    for name, (base, spread) in spreads.items():
        noise = np.random.default_rng([zlib.crc32(name.encode()), seed]).standard_normal(out[name].shape)
        drawn = base * np.exp(spread * noise) if base else spread * noise
        out[name] = jnp.asarray(drawn.astype(out[name].dtype))
    for name, factor in factors.items():
        out[name] = (out[name] * factor).astype(out[name].dtype)
    return out
```

```python
import numpy as np
import concourse.bass as bass
from concourse import mybir
from contextlib import ExitStack

F32, F32R, BF16, I32 = mybir.dt.float32, mybir.dt.float32r, mybir.dt.bfloat16, mybir.dt.int32
ALU = mybir.AluOpType
ACT = mybir.ActivationFunctionType
AX = mybir.AxisListType

P = 128
B, S, DIM = 16, 256, 512
H, HD = 4, 128
NT = B * S // P
KC = DIM // P
E, INT = 8, 352
NB = E + 2
IP = 384
IC = IP // P
NJ = 2 * B * S // P + E
TA = 10
LN_EPS, GN_EPS = 1e-5, 1e-3


def wait(e, sem, count):
    if isinstance(count, int) and count <= 0:
        return
    e.wait_ge(sem, count)


def wait_alone(e, sem, count, passed):
    wait(e, sem, count)
    e.sem_inc(passed, 1)


def pairs(e, n, peel, step):
    for t in range(peel):
        step(t, t % 2)
    with e.Fori(0, (n - 2 * peel) // 2) as i:
        step(2 * i + peel, 0)
        step(2 * i + peel + 1, 1)
    for t in range(n - peel, n):
        step(t, t % 2)


def is_between(t, lo, hi):
    return not isinstance(t, int) or lo <= t < hi


def scores_stage(nc, io, keep):
    ctx = ExitStack()
    with ctx:
        def sb(name, shape, dt):
            return ctx.enter_context(nc.sbuf_tensor(name, shape, dt))

        def pb(name, shape):
            return ctx.enter_context(nc.psum_tensor(name, shape, F32))

        def sem(name):
            return ctx.enter_context(nc.semaphore(name))

        ident, at_hi, at_lo, gates = keep["ident"], keep["at_hi"], keep["at_lo"], keep["gates"]
        x_in = sb("x_in", [P, 2, 2, DIM], F32)
        xn = sb("xn", [P, 2, 2, DIM], F32)
        xt_hi = sb("xt_hi", [P, 2, 2, KC, P], F32R)
        xt_lo = sb("xt_lo", [P, 2, 2, KC, P], F32R)
        ct_in = sb("ct_in", [P, 2, H, S], F32)
        ct_hi = sb("ct_hi", [P, 2, H, S], F32R)
        ct_lo = sb("ct_lo", [P, 2, H, S], F32R)
        q_hi = sb("q_hi", [P, H, S], F32R)
        q_lo = sb("q_lo", [P, H, S], F32R)
        w_out = sb("w_out", [P, 2, DIM], F32)
        wg_hi = sb("wg_hi", [P, KC, DIM], F32R)
        wg_lo = sb("wg_lo", [P, KC, DIM], F32R)
        g_hi = sb("g_hi", [P, H, HD], F32R)
        g_lo = sb("g_lo", [P, H, HD], F32R)
        wht = sb("wht", [P, H, HD], F32)
        zeros = sb("zeros", [P, DIM], BF16)
        stats = sb("stats", [P, 2, 2, 6], F32)
        mv = sb("mv", [P, 2, 2, 2], F32)
        sd = sb("sd", [P, 2, 2], F32)
        rstd = sb("rstd", [P, 2, 2], F32)
        eps = sb("eps", [P, 1], F32)
        decay = sb("decay", [P, 3, DIM], F32)
        wg_in = sb("wg_in", [P, KC, DIM], F32)
        masked = sb("masked", [P, 3, DIM], F32)
        stage = sb("stage", [P, 2, 2 * INT], F32)

        s_ps = pb("s_ps", [P, 3, DIM])
        t_ps = pb("t_ps", [P, 2, DIM])
        q_ps = pb("q_ps", [P, 2, DIM])
        w_ps = pb("w_ps", [P, DIM])

        consts_in, wg_loaded, decay_loaded = sem("consts_in"), sem("wg_loaded"), sem("decay_loaded")
        x_loaded = [sem("x_loaded0"), sem("x_loaded1")]
        ct_loaded = [sem("ct_loaded0"), sem("ct_loaded1")]
        gate_store = [sem("gate_store0"), sem("gate_store1")]
        g_made, g_high, g_split = sem("g_made"), sem("g_high"), sem("g_split")
        wg_high, wg_split, eps_set, zero_set = sem("wg_high"), sem("wg_split"), sem("eps_set"), sem("zero_set")
        chain, var_ready, sd_ready, xn_ready = sem("chain"), sem("var_ready"), sem("sd_ready"), sem("xn_ready")
        xt_made, xt_high, xt_low = sem("xt_made"), sem("xt_high"), sem("xt_low")
        q_made, q_high, q_low = sem("q_made"), sem("q_high"), sem("q_low")
        ct_high, ct_low = sem("ct_high"), sem("ct_low")
        gate_made, gate_relu, s_added = sem("gate_made"), sem("gate_relu"), sem("s_added")
        a_ready, a_high, upper_set = sem("a_ready"), sem("a_high"), sem("upper_set")
        a_split = sem("a_split")
        stage_loaded = [sem("stage_loaded0"), sem("stage_loaded1")]
        pool_chain, tanh_done, passed = sem("pool_chain"), sem("tanh_done"), sem("passed")
        block = ctx.enter_context(nc.Block())

        def bank(t, i):
            return t[:, i, :]

        def a_part(t, i):
            return t[:, 2 * i:2 * i + 2, 0, :] if i < 2 else t[:, :, 1, P:S]

        def masked_part(i):
            return masked[:, i, :].rearrange("p (h s) -> p h s", h=2 if i < 2 else H)

        @block.sync
        def _(sp):
            sp.dma_start(wht[:, :, :], io["wht"]).then_inc(consts_in, 16)
            sp.dma_start(ident[:, :], io["ident"]).then_inc(consts_in, 16)
            sp.dma_start(gates[:, 0:2], io["gates"]).then_inc(consts_in, 16)

            def step(b, k):
                wait(sp, xn_ready, b - 1)
                sp.dma_start(x_in[:, k, :, :], io["x_batch"](b)).then_inc(x_loaded[k], 16)
                wait(sp, ct_low, b - 1)
                sp.dma_start(ct_in[:, k, :, :], io["ct_batch"](b)).then_inc(ct_loaded[k], 16)
                if isinstance(b, int) and b == 0:
                    sp.dma_start(wg_in[:, :, :], io["wg"]).then_inc(wg_loaded, 16)
                    sp.dma_start(decay[:, :, :], io["decay"]).then_inc(decay_loaded, 16)

            pairs(sp, B, 2, step)
            for q in range(2):
                sp.wait_ge(gate_store[q], 16 * B)

        @block.scalar
        def _(act):
            act.wait_ge(consts_in, 48)
            act.activation(gates[:, 2:4], gates[:, 0:2], ACT.Tanh).then_inc(tanh_done, 1)
            act.wait_ge(eps_set, 1)

            def root(b, k):
                act.wait_ge(var_ready, b + 1)
                act.activation(sd[:, k, :], mv[:, k, :, 1], ACT.Sqrt, bias=eps[:, 0:1]).then_inc(sd_ready, 1)

            def xt_high_part(b, k):
                for q in range(2):
                    act.wait_ge(xt_made, 2 * b + q + 1)
                    wait(act, gate_made, 2 * b - 2)
                    act.activation(xt_hi[:, k, q, :, :], bank(t_ps, q).rearrange("p (k t) -> p k t", k=KC),
                                   ACT.Copy).then_inc(xt_high, 1)

            def ct_high_part(b, k):
                act.wait_ge(ct_loaded[k], 16 * (b // 2) + 16 if isinstance(b, int) else (b - k) * 8 + 16)
                wait(act, s_added, b - 1)
                act.activation(ct_hi[:, k, :, :], ct_in[:, k, :, :], ACT.Copy).then_inc(ct_high, 1)

            root(0, 0)
            act.wait_ge(g_made, 1)
            act.activation(g_hi[:, :, :], bank(q_ps, 0).rearrange("p (h d) -> p h d", h=H), ACT.Copy).then_inc(g_high, 1)
            ct_high_part(0, 0)
            xt_high_part(0, 0)
            root(1, 1)
            act.wait_ge(wg_loaded, 16)
            act.activation(wg_hi[:, :, :], wg_in[:, :, :], ACT.Copy).then_inc(wg_high, 1)

            def step(b, k):
                for i in range(2):
                    act.wait_ge(q_made, 2 * b + i + 1)
                    wait(act, s_added, b)
                    act.activation(q_hi[:, 2 * i:2 * i + 2, :], bank(q_ps, i).rearrange("p (h s) -> p h s", h=2),
                                   ACT.Copy).then_inc(q_high, 1)
                if is_between(b, 0, B - 1):
                    xt_high_part(b + 1, 1 - k)
                    ct_high_part(b + 1, 1 - k)
                if is_between(b, 0, B - 2):
                    root(b + 2, k)
                for q in range(2):
                    act.wait_ge(gate_made, 2 * b + q + 1)
                    wait(act, gate_store[q], 16 * b)
                    act.activation(w_out[:, q, :], w_ps[:, :], ACT.Relu).then_inc(gate_relu, 1)
                    act.wait_ge(gate_relu, 2 * b + q + 1)
                    act.dma_start(io["gate_tile"](b, q), w_out[:, q, :]).then_inc(gate_store[q], 16)

            pairs(act, B, 2, step)
            for i in range(3):
                act.wait_ge(a_ready, i + 1)
                act.activation(a_part(at_hi, i), masked_part(i), ACT.Copy).then_inc(a_high, 1)

        @block.vector
        def _(dve):
            links = [0]

            def link(ins):
                links[0] += 1
                ins.then_inc(chain, 1)
                dve.wait_ge(chain, links[0])

            dve.memset(eps[:, :], LN_EPS).then_inc(eps_set, 1)
            dve.memset(zeros[:, :], 0.0).then_inc(zero_set, 1)

            def moments(b, k, n):
                dve.wait_ge(x_loaded[k], (b - k) * 8 + 16)
                for q in range(2):
                    ins = dve.bn_stats(stats[:, k, q, :], x_in[:, k, q, :])
                ins.then_inc(chain, 1)
                wait_alone(dve, chain, n + 1, passed)
                for q in range(2):
                    ins = dve.bn_aggr(mv[:, k, q, :], stats[:, k, q, :])
                ins.then_inc(var_ready, 1)

            def normalise(b, k, n):
                dve.wait_ge(sd_ready, b + 1)
                dve.reciprocal(rstd[:, k, :], sd[:, k, :]).then_inc(chain, 1)
                dve.wait_ge(chain, n + 2)
                wait(dve, xt_made, 2 * b - 2)
                for q in range(2):
                    ins = dve.tensor_scalar(xn[:, k, q, :], x_in[:, k, q, :], mv[:, k, q, 0:1],
                                            rstd[:, k, q:q + 1], ALU.subtract, ALU.mult)
                ins.then_inc(xn_ready, 1)

            def xt_low_part(b, k):
                for q in range(2):
                    dve.wait_ge(xt_high, 2 * b + q + 1)
                    dve.tensor_tensor(xt_lo[:, k, q, :, :], bank(t_ps, q).rearrange("p (k t) -> p k t", k=KC),
                                      xt_hi[:, k, q, :, :].bitcast(F32), ALU.subtract).then_inc(xt_low, 1)

            def ct_low_part(b, k):
                dve.wait_ge(ct_high, b + 1)
                dve.tensor_tensor(ct_lo[:, k, :, :], ct_in[:, k, :, :], ct_hi[:, k, :, :].bitcast(F32),
                                  ALU.subtract).then_inc(ct_low, 1)

            moments(0, 0, 0)
            normalise(0, 0, 0)
            dve.wait_ge(g_high, 1)
            dve.tensor_tensor(g_lo[:, :, :], bank(q_ps, 0).rearrange("p (h d) -> p h d", h=H),
                              g_hi[:, :, :].bitcast(F32), ALU.subtract).then_inc(g_split, 1)
            ct_low_part(0, 0)
            xt_low_part(0, 0)
            moments(1, 1, 2)
            normalise(1, 1, 2)
            dve.wait_ge(wg_high, 1)
            dve.tensor_tensor(wg_lo[:, :, :], wg_in[:, :, :], wg_hi[:, :, :].bitcast(F32),
                              ALU.subtract).then_inc(wg_split, 1)

            def step(b, k):
                if is_between(b, 0, B - 2):
                    moments(b + 2, k, 2 * b + 4)
                for i in range(2):
                    dve.wait_ge(q_high, 2 * b + i + 1)
                    dve.tensor_tensor(q_lo[:, 2 * i:2 * i + 2, :], bank(q_ps, i).rearrange("p (h s) -> p h s", h=2),
                                      q_hi[:, 2 * i:2 * i + 2, :].bitcast(F32), ALU.subtract).then_inc(q_low, 1)
                if is_between(b, 0, B - 1):
                    xt_low_part(b + 1, 1 - k)
                    ct_low_part(b + 1, 1 - k)
                if is_between(b, 0, B - 2):
                    normalise(b + 2, k, 2 * b + 4)

            pairs(dve, B, 2, step)
            links[0] = 2 * B
            dve.wait_ge(decay_loaded, 16)
            dve.wait_ge(s_added, B)
            for i in range(3):
                m = masked[:, i, :]
                link(dve.tensor_tensor(m, bank(s_ps, i), decay[:, i, :], ALU.mult))
                link(dve.scalar_tensor_tensor(out=m, in0=m, scalar=-1.0, in1=m, op0=ALU.mult, op1=ALU.max))
                dve.tensor_scalar(m, m, 1.0, None, ALU.max).then_inc(a_ready, 1)
            for i in range(3):
                dve.wait_ge(a_high, i + 1)
                dve.tensor_tensor(a_part(at_lo, i), masked_part(i), a_part(at_hi, i).bitcast(F32),
                                  ALU.subtract).then_inc(a_split, 1)

        @block.gpsimd
        def _(pool):
            links = [0]

            def link(ins):
                links[0] += 1
                ins.then_inc(pool_chain, 1)
                pool.wait_ge(pool_chain, links[0])

            pool.memset(at_hi[:, :, 1, 0:P].bitcast(F32), 1.0).then_inc(upper_set, 1)
            pool.memset(at_lo[:, :, 1, 0:P].bitcast(F32), 0.0).then_inc(upper_set, 1)
            keep["gu_sh_chunks"](pool, stage, stage_loaded, link)

        @block.tensor
        def _(pe):
            pe.wait_ge(consts_in, 48)
            for h in range(H):
                mm = pe.matmul(q_ps[:, 0, h * HD:(h + 1) * HD], wht[:, h, :], wht[:, h, :], start=True, stop=True)
            mm.then_inc(g_made, 1)
            pe.wait_ge(zero_set, 1)
            for i in range(3):
                pe.matmul(bank(s_ps, i), zeros[:, 0:P], zeros[:, :], start=True, stop=False, skip_group_check=True)

            def turn(b, k):
                pe.wait_ge(xn_ready, b + 1)
                for q in range(2):
                    wait(pe, xt_low, 2 * b + q - 1)
                    for c in range(KC):
                        mm = pe.transpose(t_ps[:, q, c * P:(c + 1) * P], xn[:, k, q, c * P:(c + 1) * P], ident[:, :])
                    mm.then_inc(xt_made, 1)

            def gate(b, k, q):
                wait(pe, gate_relu, 2 * b + q)
                for c in range(KC):
                    for n, (a, w) in enumerate(((xt_hi, wg_hi), (xt_hi, wg_lo), (xt_lo, wg_hi))):
                        mm = pe.matmul(w_ps[:, :], a[:, k, q, c, :], w[:, c, :], start=(c == 0 and n == 0),
                                       stop=(c == KC - 1 and n == 2))
                mm.then_inc(gate_made, 1)

            turn(0, 0)
            pe.wait_ge(g_split, 1)

            def step(b, k):
                pe.wait_ge(xt_high, 2 * b + 2)
                pe.wait_ge(xt_low, 2 * b + 2)
                for i in range(2):
                    wait(pe, q_low, 2 * b + i - 1)
                    for h in (2 * i, 2 * i + 1):
                        out = q_ps[:, i, (h % 2) * S:(h % 2 + 1) * S]
                        for n, (g, a) in enumerate(((g_hi, xt_hi), (g_hi, xt_lo), (g_lo, xt_hi))):
                            mm = pe.matmul(out, g[:, h, :], a[:, k, :, h, :], start=(n == 0), stop=(n == 2))
                    mm.then_inc(q_made, 1)
                if is_between(b, 0, B - 1):
                    turn(b + 1, 1 - k)
                if isinstance(b, int) and b == 0:
                    pe.wait_ge(wg_split, 1)
                gate(b, k, 0)
                pe.wait_ge(q_high, 2 * b + 2)
                pe.wait_ge(q_low, 2 * b + 2)
                pe.wait_ge(ct_high, b + 1)
                pe.wait_ge(ct_low, b + 1)
                for h in range(H):
                    for kt in range(2):
                        out = s_ps[:, h // 2, (h % 2) * S:(h % 2 + 1) * S] if kt == 0 else s_ps[:, 2, h * P:(h + 1) * P]
                        for c, a in ((ct_hi, q_hi), (ct_hi, q_lo), (ct_lo, q_hi)):
                            mm = pe.matmul(out, c[:, k, h, kt * P:(kt + 1) * P], a[:, h, kt * P:S], start=False,
                                           stop=False, skip_group_check=True)
                mm.then_inc(s_added, 1)
                gate(b, k, 1)

            pairs(pe, B, 2, step)


def shared_weights(pool, io, keep, stage, stage_loaded, link):
    wu_hi, wu_lo, wd_hi, wd_lo = (keep[n] for n in ("shu_hi", "shu_lo", "shd_hi", "shd_lo"))
    link(pool.memset(wd_hi[:, :, IC - 1, :], 0.0))
    link(pool.memset(wd_lo[:, :, IC - 1, :], 0.0))

    def chunk(n):
        blk, c = n // (KC + IC), n % (KC + IC)
        if c < KC:
            return stage[:, n % 2, :], io["gu"][E + blk, :, c, :], wu_hi[:, blk, c, :], wu_lo[:, blk, c, :]
        i = c - KC
        rows = min(P, INT - i * P)
        return (stage[0:rows, n % 2, 0:DIM], io["down"][E + blk, i * P:i * P + rows, :],
                wd_hi[0:rows, blk, i, :], wd_lo[0:rows, blk, i, :])

    def load(n):
        s, dram, _, _ = chunk(n)
        pool.dma_start(s, dram).then_inc(stage_loaded[n % 2], 16)

    total = 2 * (KC + IC)
    load(0)
    load(1)
    for n in range(total):
        s, _, hi, lo = chunk(n)
        pool.wait_ge(stage_loaded[n % 2], 16 * (n // 2 + 1))
        link(pool.tensor_scalar(hi, s, 1.0, None, ALU.mult))
        link(pool.tensor_tensor(lo, s, hi, ALU.subtract))
        if n + 2 < total:
            load(n + 2)


def mix_stage(nc, io, keep):
    ctx = ExitStack()
    with ctx:
        def sb(name, shape, dt):
            return ctx.enter_context(nc.sbuf_tensor(name, shape, dt))

        def pb(name, shape):
            return ctx.enter_context(nc.psum_tensor(name, shape, F32))

        def sem(name):
            return ctx.enter_context(nc.semaphore(name))

        ident, at_hi, at_lo, gates, logits = (keep[n] for n in ("ident", "at_hi", "at_lo", "gates", "logits"))
        c_in = sb("c_in", [P, 2, 2, DIM], F32)
        c_hi = sb("c_hi", [P, 2, 2, DIM], F32R)
        c_lo = sb("c_lo", [P, 2, 2, DIM], F32R)
        x_in = sb("x2_in", [P, 2, 2, DIM], F32)
        w_in = sb("w_in", [P, 2, 2, DIM], F32)
        u_hi = sb("u_hi", [P, H, S], F32R)
        u_lo = sb("u_lo", [P, H, S], F32R)
        nrm = sb("nrm", [P, 2, DIM], F32)
        z = sb("z", [P, 2, 2, DIM], F32)
        zt_hi = sb("zt_hi", [P, 2, KC, P], F32R)
        zt_lo = sb("zt_lo", [P, 2, KC, P], F32R)
        x1 = sb("x1", [P, 2, DIM], F32)
        xn = sb("xn2", [P, 2, DIM], F32)
        xt = sb("xt_f", [P, 2, DIM], F32)
        xt16 = sb("xt16", [P, 2, 2, DIM], BF16)
        wh = sb("wh", [P, H, HD], F32)
        wh_hi = sb("wh_hi", [P, H, HD], F32R)
        wh_lo = sb("wh_lo", [P, H, HD], F32R)
        wo = sb("wo", [P, KC, DIM], F32)
        wo_hi = sb("wo_hi", [P, KC, DIM], F32R)
        wo_lo = sb("wo_lo", [P, KC, DIM], F32R)
        wr = sb("wr", [P, KC, E], F32)
        affine = sb("affine", [P, 2, DIM], F32)
        o_stats = sb("o_stats", [P, 2, 6], F32)
        o_mv = sb("o_mv", [P, 2, 2], F32)
        o_sd = sb("o_sd", [P, 2], F32)
        o_rstd = sb("o_rstd", [P, 2, 2], F32)
        x_stats = sb("x_stats", [P, 2, 6], F32)
        x_mv = sb("x_mv", [P, 2, 2], F32)
        x_sd = sb("x_sd", [P, 2], F32)
        x_rstd = sb("x_rstd", [P, 2, 2], F32)
        eps = sb("eps2", [P, 2], F32)

        u_ps = pb("u_ps", [P, 2, DIM])
        o_ps = pb("o_ps", [P, 2, DIM])
        t_ps = pb("t2_ps", [P, 2, DIM])
        y_ps = pb("y_ps", [P, 2, DIM])

        def two(name):
            return [sem(name + "0"), sem(name + "1")]

        consts_in, weights_high, weights_split, eps_set = (
            sem("consts2_in"), sem("weights_high"), sem("weights_split"), sem("eps2_set"))
        c_loaded, x_loaded, w_loaded = two("c_loaded"), two("x2_loaded"), two("w_loaded")
        c_high, c_low, u_made, u_high, u_low = (sem("c_high"), sem("c_low"), sem("u_made"), sem("u_high"), sem("u_low"))
        o_made, o_var, o_root, o_scale, n_ready, z_ready = (
            sem("o_made"), sem("o_var"), sem("o_root"), sem("o_scale"), sem("n_ready"), sem("z_ready"))
        zt_made, zt_high, zt_low, y_made, x1_ready = (
            sem("zt_made"), sem("zt_high"), sem("zt_low"), sem("y_made"), sem("x1_ready"))
        x_var, x_root, x_scale, xn_ready = sem("x_var"), sem("x_root"), sem("x_scale"), sem("xn2_ready")
        xt_made, xt_copied, xt_high, xt_low = sem("xt2_made"), sem("xt_copied"), sem("xt2_high"), sem("xt2_low")
        r_made, r_kept, chain, pool_chain = sem("r_made"), sem("r_kept"), sem("chain2"), sem("pool_chain2")
        passed = sem("passed2")
        x1_store, xn_store, xt_store = two("x1_store"), two("xn_store"), two("xt_store")
        block = ctx.enter_context(nc.Block())

        def batches(e, step):
            for b in range(4):
                step(b, b % 2)
            with e.Fori(0, (B - 6) // 2) as i:
                step(2 * i + 4, 0)
                step(2 * i + 5, 1)
            for b in range(B - 2, B + 2):
                step(b, b % 2)

        @block.sync
        def _(sp):
            for t, name in ((wh, "wh"), (wo, "wo")):
                sp.dma_start(t[:, :, :], io[name]).then_inc(consts_in, 16)
            sp.dma_start(c_in[:, 0, :, :], io["c_batch"](0)).then_inc(c_loaded[0], 16)
            sp.dma_start(c_in[:, 1, :, :], io["c_batch"](1)).then_inc(c_loaded[1], 16)
            sp.dma_start(wr[:, :, :], io["wr"]).then_inc(consts_in, 16)
            sp.dma_start(affine[:, :, :], io["affine"]).then_inc(consts_in, 16)
            sp.dma_start(w_in[:, 0, :, :], io["gate_batch"](0)).then_inc(w_loaded[0], 16)

            def stores(b, q):
                sp.wait_ge(xn_ready, 2 * b + q + 1)
                sp.dma_start(io["x1_tile"](b, q), x1[:, q, :]).then_inc(x1_store[q], 16)
                sp.dma_start(io["xn_tile"](b, q), xn[:, q, :]).then_inc(xn_store[q], 16)

            def step(b, k):
                if is_between(b, 0, B - 1):
                    wait(sp, z_ready, 2 * b)
                    sp.dma_start(w_in[:, 1 - k, :, :], io["gate_batch"](b + 1)).then_inc(w_loaded[1 - k], 16)
                if is_between(b, 0, B):
                    wait(sp, x1_ready, 2 * b - 2)
                    sp.dma_start(x_in[:, k, :, :], io["x_batch"](b)).then_inc(x_loaded[k], 16)
                if is_between(b, 0, B - 2):
                    sp.wait_ge(c_low, b + 1)
                    sp.dma_start(c_in[:, k, :, :], io["c_batch"](b + 2)).then_inc(c_loaded[k], 16)
                if is_between(b - 2, 0, B):
                    stores(b - 2, 1)
                    for q in range(2):
                        sp.wait_ge(xt_low, 2 * (b - 2) + q + 1)
                        sp.dma_start(io["xt_tile"](b - 2, q), xt16[:, q, :, :]).then_inc(xt_store[q], 16)
                if is_between(b - 1, 0, B):
                    stores(b - 1, 0)

            batches(sp, step)
            for s in x1_store + xn_store + xt_store:
                sp.wait_ge(s, 16 * B)

        @block.scalar
        def _(act):
            act.wait_ge(consts_in, 64)
            act.activation(wh_hi[:, :, :], wh[:, :, :], ACT.Copy).then_inc(weights_high, 1)
            act.wait_ge(eps_set, 2)

            def c_high_part(b, k):
                act.wait_ge(c_loaded[k], (b - k) * 8 + 16)
                wait(act, u_made, 2 * b - 2)
                act.activation(c_hi[:, k, :, :], c_in[:, k, :, :], ACT.Copy).then_inc(c_high, 1)

            def u_high_part(b):
                for i in range(2):
                    act.wait_ge(u_made, 2 * b + i + 1)
                    wait(act, o_made, 2 * b)
                    act.activation(u_hi[:, 2 * i:2 * i + 2, :], u_ps[:, i, :].rearrange("p (h s) -> p h s", h=2),
                                   ACT.Copy).then_inc(u_high, 1)

            def norm_o(b, q):
                act.wait_ge(o_var, 2 * b + q + 1)
                act.activation(o_sd[:, q:q + 1], o_mv[:, q, 1:2], ACT.Sqrt, bias=eps[:, 1:2]).then_inc(o_root, 1)
                act.wait_ge(o_scale, 2 * b + q + 1)
                wait(act, z_ready, 2 * b + q - 1)
                act.activation(nrm[:, q, :], o_ps[:, q, :], ACT.Identity, bias=o_rstd[:, q, 1:2],
                               scale=o_rstd[:, q, 0:1]).then_inc(n_ready, 1)

            def norm_x(b, q):
                act.wait_ge(x_var, 2 * b + q + 1)
                act.activation(x_sd[:, q:q + 1], x_mv[:, q, 1:2], ACT.Sqrt, bias=eps[:, 0:1]).then_inc(x_root, 1)
                act.wait_ge(x_scale, 2 * b + q + 1)
                wait(act, xt_made, 2 * b + q - 1)
                wait(act, xn_store[q], 16 * b)
                act.activation(xn[:, q, :], x1[:, q, :], ACT.Identity, bias=x_rstd[:, q, 1:2],
                               scale=x_rstd[:, q, 0:1]).then_inc(xn_ready, 1)

            c_high_part(0, 0)
            c_high_part(1, 1)
            u_high_part(0)
            act.activation(wo_hi[:, :, :], wo[:, :, :], ACT.Copy).then_inc(weights_high, 1)

            def step(b, k):
                if is_between(b - 2, 0, B):
                    norm_x(b - 2, 1)
                if is_between(b, 0, B):
                    norm_o(b, 0)
                    norm_o(b, 1)
                if is_between(b - 2, 0, B):
                    for q in range(2):
                        act.wait_ge(xt_made, 2 * (b - 2) + q + 1)
                        wait(act, xt_low, 2 * (b - 2) + q - 1)
                        act.activation(xt[:, q, :], t_ps[:, q, :], ACT.Copy).then_inc(xt_copied, 1)
                if is_between(b - 1, 0, B):
                    for q in range(2):
                        act.wait_ge(zt_made, 2 * (b - 1) + q + 1)
                        wait(act, y_made, 2 * (b - 2) + q + 1)
                        act.activation(zt_hi[:, q, :, :], y_ps[:, q, :].rearrange("p (k t) -> p k t", k=KC),
                                       ACT.Copy).then_inc(zt_high, 1)
                if is_between(b - 2, 0, B):
                    for q in range(2):
                        act.wait_ge(xt_copied, 2 * (b - 2) + q + 1)
                        wait(act, xt_store[q], 16 * (b - 2))
                        act.activation(xt16[:, q, 0, :], xt[:, q, :], ACT.Copy).then_inc(xt_high, 1)
                if is_between(b, 0, B - 1):
                    u_high_part(b + 1)
                if is_between(b, 0, B - 2):
                    c_high_part(b + 2, k)
                if is_between(b - 1, 0, B):
                    norm_x(b - 1, 0)

            batches(act, step)

        @block.vector
        def _(dve):
            dve.memset(eps[:, 0:1], LN_EPS).then_inc(eps_set, 1)
            dve.memset(eps[:, 1:2], GN_EPS).then_inc(eps_set, 1)
            dve.wait_ge(weights_high, 1)
            dve.tensor_tensor(wh_lo[:, :, :], wh[:, :, :], wh_hi[:, :, :].bitcast(F32),
                              ALU.subtract).then_inc(weights_split, 1)
            LINKS = 2

            def norm(src, stats, mv, sd, rstd, var, root, scale, n, i, q):
                dve.bn_stats(stats[:, q, :], src).then_inc(chain, 1)
                wait_alone(dve, chain, n + 1, passed)
                dve.bn_aggr(mv[:, q, :], stats[:, q, :]).then_inc(var, 1)
                dve.wait_ge(root, i + 1)
                dve.reciprocal(rstd[:, q, 0:1], sd[:, q:q + 1]).then_inc(chain, 1)
                dve.wait_ge(chain, n + LINKS)
                dve.scalar_tensor_tensor(out=rstd[:, q, 1:2], in0=mv[:, q, 0:1], scalar=-1.0, in1=rstd[:, q, 0:1],
                                         op0=ALU.mult, op1=ALU.mult).then_inc(scale, 1)

            def norm_o(b, q, n):
                dve.wait_ge(o_made, 2 * b + q + 1)
                norm(o_ps[:, q, :], o_stats, o_mv, o_sd, o_rstd, o_var, o_root, o_scale, n, 2 * b + q, q)

            def residual(b, q, n):
                dve.wait_ge(y_made, 2 * b + q + 1)
                dve.wait_ge(x_loaded[kof(b, q)], xcount(b))
                wait(dve, x1_store[q], 16 * b)
                wait(dve, xn_ready, 2 * b + q - 1)
                dve.scalar_tensor_tensor(out=x1[:, q, :], in0=y_ps[:, q, :], scalar=gates[:, 2:3],
                                         in1=x_in[:, kof(b, q), q, :], op0=ALU.mult,
                                         op1=ALU.add).then_inc(x1_ready, 1)
                dve.wait_ge(x1_ready, 2 * b + q + 1)
                norm(x1[:, q, :], x_stats, x_mv, x_sd, x_rstd, x_var, x_root, x_scale, n, 2 * b + q, q)

            parity = [0]

            def kof(b, q):
                return parity[0]

            def xcount(b):
                return (b - parity[0]) * 8 + 16

            def u_low_part(b):
                for i in range(2):
                    dve.wait_ge(u_high, 2 * b + i + 1)
                    dve.tensor_tensor(u_lo[:, 2 * i:2 * i + 2, :], u_ps[:, i, :].rearrange("p (h s) -> p h s", h=2),
                                      u_hi[:, 2 * i:2 * i + 2, :].bitcast(F32), ALU.subtract).then_inc(u_low, 1)

            u_low_part(0)
            dve.wait_ge(weights_high, 2)
            dve.tensor_tensor(wo_lo[:, :, :], wo[:, :, :], wo_hi[:, :, :].bitcast(F32),
                              ALU.subtract).then_inc(weights_split, 1)

            def step(b, k):
                if is_between(b - 2, 0, B):
                    parity[0] = k
                    residual(b - 2, 1, LINKS * links_before(b, 0))
                if is_between(b, 0, B):
                    norm_o(b, 0, LINKS * links_before(b, 1))
                    norm_o(b, 1, LINKS * links_before(b, 2))
                if is_between(b - 1, 0, B):
                    for q in range(2):
                        dve.wait_ge(zt_high, 2 * (b - 1) + q + 1)
                        dve.tensor_tensor(zt_lo[:, q, :, :], y_ps[:, q, :].rearrange("p (k t) -> p k t", k=KC),
                                          zt_hi[:, q, :, :].bitcast(F32), ALU.subtract).then_inc(zt_low, 1)
                if is_between(b, 0, B - 1):
                    u_low_part(b + 1)
                if is_between(b - 2, 0, B):
                    for q in range(2):
                        dve.wait_ge(r_made, 2 * (b - 2) + q + 1)
                        dve.tensor_copy(logits_of(b - 2, q), t_ps[:, q, 0:E]).then_inc(r_kept, 1)
                    for q in range(2):
                        dve.wait_ge(xt_high, 2 * (b - 2) + q + 1)
                        dve.tensor_tensor(xt16[:, q, 1, :], xt[:, q, :], xt16[:, q, 0, :],
                                          ALU.subtract).then_inc(xt_low, 1)
                if is_between(b - 1, 0, B):
                    parity[0] = 1 - k
                    residual(b - 1, 0, LINKS * links_before(b, 3))

            def logits_of(b, q):
                t = 2 * b + q
                return logits[:, t, :] if isinstance(t, int) else logits[:, bass.ds(t, 1), :].rearrange("p a e -> p (a e)")

            def links_before(b, part):
                if not isinstance(b, int):
                    return 4 * b - 3 + part
                done = 0
                for s in range(b + 1):
                    for i, there in enumerate((0 <= s - 2 < B, s < B, s < B, 0 <= s - 1 < B)):
                        if s == b and i == part:
                            return done
                        done += there
                return done

            batches(dve, step)

        @block.gpsimd
        def _(pool):
            def c_low_part(b, k):
                pool.wait_ge(c_high, b + 1)
                pool.tensor_tensor(c_lo[:, k, :, :], c_in[:, k, :, :], c_hi[:, k, :, :].bitcast(F32),
                                   ALU.subtract).then_inc(c_low, 1)

            c_low_part(0, 0)
            c_low_part(1, 1)
            pool.wait_ge(consts_in, 64)

            def step(b, k):
                if is_between(b, 0, B):
                    for q in range(2):
                        i = 2 * b + q
                        pool.wait_ge(n_ready, i + 1)
                        pool.tensor_tensor(nrm[:, q, :], nrm[:, q, :], affine[:, 0, :], ALU.mult).then_inc(pool_chain, 1)
                        pool.wait_ge(pool_chain, 2 * i + 1)
                        pool.tensor_tensor(nrm[:, q, :], nrm[:, q, :], affine[:, 1, :], ALU.add).then_inc(pool_chain, 1)
                        pool.wait_ge(pool_chain, 2 * i + 2)
                        pool.wait_ge(w_loaded[k], (b - k) * 8 + 16)
                        wait(pool, zt_made, i - 3)
                        pool.tensor_tensor(z[:, k, q, :], nrm[:, q, :], w_in[:, k, q, :], ALU.mult).then_inc(z_ready, 1)
                if is_between(b, 0, B - 2):
                    c_low_part(b + 2, k)

            batches(pool, step)

        @block.tensor
        def _(pe):
            pe.wait_ge(consts_in, 64)

            def attend(b, k):
                pe.wait_ge(c_high, b + 1)
                pe.wait_ge(c_low, b + 1)
                for i in range(2):
                    wait(pe, u_low, 2 * b + i - 1)
                    for h in (2 * i, 2 * i + 1):
                        n = 0
                        for kt in range(2):
                            for c, a in ((c_hi, at_hi), (c_hi, at_lo), (c_lo, at_hi)):
                                mm = pe.matmul(u_ps[:, i, (h % 2) * S:(h % 2 + 1) * S], c[:, k, kt, h * HD:(h + 1) * HD],
                                               a[:, h, kt, :], start=(n == 0), stop=(n == 5))
                                n += 1
                    mm.then_inc(u_made, 1)

            attend(0, 0)
            pe.wait_ge(weights_split, 2)

            def step(b, k):
                if is_between(b, 0, B):
                    pe.wait_ge(u_high, 2 * b + 2)
                    pe.wait_ge(u_low, 2 * b + 2)
                    for q in range(2):
                        wait(pe, n_ready, 2 * b + q - 1)
                        for h in range(H):
                            for n, (a, w) in enumerate(((u_hi, wh_hi), (u_hi, wh_lo), (u_lo, wh_hi))):
                                mm = pe.matmul(o_ps[:, q, h * HD:(h + 1) * HD], a[:, h, q * P:(q + 1) * P], w[:, h, :],
                                               start=(n == 0), stop=(n == 2))
                        mm.then_inc(o_made, 1)
                if is_between(b - 2, 0, B):
                    for q in range(2):
                        pe.wait_ge(xn_ready, 2 * (b - 2) + q + 1)
                        wait(pe, r_kept, 2 * (b - 3) + q + 1)
                        for c in range(KC):
                            mm = pe.transpose(t_ps[:, q, c * P:(c + 1) * P], xn[:, q, c * P:(c + 1) * P], ident[:, :])
                        mm.then_inc(xt_made, 1)
                if is_between(b - 1, 0, B):
                    for q in range(2):
                        pe.wait_ge(z_ready, 2 * (b - 1) + q + 1)
                        wait(pe, x1_ready, 2 * (b - 2) + q + 1)
                        for c in range(KC):
                            mm = pe.transpose(y_ps[:, q, c * P:(c + 1) * P], z[:, 1 - k, q, c * P:(c + 1) * P], ident[:, :])
                        mm.then_inc(zt_made, 1)
                if is_between(b, 0, B - 1):
                    attend(b + 1, 1 - k)
                if is_between(b - 2, 0, B):
                    for q in range(2):
                        pe.wait_ge(xt_copied, 2 * (b - 2) + q + 1)
                        for c in range(KC):
                            mm = pe.matmul(t_ps[:, q, 0:E], xt[:, q, c * P:(c + 1) * P], wr[:, c, :], start=(c == 0),
                                           stop=(c == KC - 1))
                        mm.then_inc(r_made, 1)
                if is_between(b - 1, 0, B):
                    for q in range(2):
                        pe.wait_ge(zt_low, 2 * (b - 1) + q + 1)
                        pe.wait_ge(zt_high, 2 * (b - 1) + q + 1)
                        for c in range(KC):
                            for n, (a, w) in enumerate(((zt_hi, wo_hi), (zt_hi, wo_lo), (zt_lo, wo_hi))):
                                mm = pe.matmul(y_ps[:, q, :], a[:, q, c, :], w[:, c, :], start=(c == 0 and n == 0),
                                               stop=(c == KC - 1 and n == 2))
                        mm.then_inc(y_made, 1)

            batches(pe, step)


def ffn_stage(nc, io, keep):
    ctx = ExitStack()
    with ctx:
        def sb(name, shape, dt):
            return ctx.enter_context(nc.sbuf_tensor(name, shape, dt))

        def pb(name, shape):
            return ctx.enter_context(nc.psum_tensor(name, shape, F32))

        def sem(name):
            return ctx.enter_context(nc.semaphore(name))

        def two(name):
            return [sem(name + "0"), sem(name + "1")]

        ident, gates, logits = keep["ident"], keep["gates"], keep["logits"]
        shu = (keep["shu_hi"], keep["shu_lo"])
        shd = (keep["shd_hi"], keep["shd_lo"])
        exu = (sb("exu_hi", [P, E, KC, 2 * INT], BF16), sb("exu_lo", [P, E, KC, 2 * INT], BF16))
        exd = (sb("exd_hi", [P, E, IC, DIM], BF16), sb("exd_lo", [P, E, IC, DIM], BF16))
        xt = sb("xt_parts", [P, 2, 2, DIM], BF16)
        silu = sb("silu", [P, 2, INT], F32)
        h = sb("h", [P, 2, IP], F32)
        ht = sb("ht_parts", [P, 2, 2, IP], BF16)
        rows = sb("rows", [P, 3, 2 * INT], F32)
        acc = sb("acc", [P, 2, DIM], F32)
        out_row = sb("out_row", [P, 2, DIM], F32)
        tri = sb("tri", [P, P], F32)
        ones = sb("ones", [P, P], F32)
        iota = sb("iota", [P, E + NJ], F32)
        token = sb("token", [P, NT], I32)
        top1, top2 = sb("top1", [P, NT, E], F32), sb("top2", [P, NT, E], F32)
        small = sb("small", [P, 8, NT], F32)
        tiles = sb("tiles", [P, 5, E], F32)
        tiles_i = sb("tiles_i", [P, 2, E], I32)
        weight = sb("weight", [P, 2, NT], F32)
        slot = sb("slot", [P, 2, NT], I32)
        slot_part = sb("slot_part", [P, 2, 2, NT], I32)
        table_at = sb("table_at", [P, 2, NT], I32)
        experts_f = sb("experts_f", [1, NJ], F32)
        experts = sb("experts", [1, NJ], I32)
        slot_token = sb("slot_token", [P, NJ], I32)
        put_at = sb("put_at", [P, 2, 2, 2], I32)
        put_token = sb("put_token", [P, 2, 2], I32)
        get_at = sb("get_at", [P, 2, 2], I32)

        flat = rows[:, :, :].rearrange("p a b -> p (a b)")
        xg = flat[:, 0:2 * DIM].rearrange("p (a b) -> p a b", a=2)
        y_out = flat[:, 2 * DIM:4 * DIM].rearrange("p (a b) -> p a b", a=2)
        y_in = flat[:, 0:4 * DIM].rearrange("p (a r b) -> p a r b", a=2, r=2)
        rank = out_row[:, 0, :].rearrange("p (a t e) -> p a t e", a=2, e=E)
        before = out_row[:, 1, 0:NT * E].rearrange("p (t e) -> p t e", e=E)
        work = out_row[:, 1, NT * E:2 * NT * E].rearrange("p (t e) -> p t e", e=E)

        slot_f = small[:, 0:4, :].rearrange("p (a r) t -> p a r t", a=2)

        gu_ps = pb("gu_ps", [P, 2, 2, DIM])
        h_ps = pb("h_ps", [P, DIM])
        x_ps = pb("x_ps", [P, DIM])
        y_ps = pb("y3_ps", [P, 2, DIM])

        consts_in, h_pad, passed = sem("consts3_in"), sem("h_pad"), sem("passed3")
        pool_zero = sem("pool_zero")
        chain, exp_in, exp_out, top_ready = sem("chain3"), sem("exp_in"), sem("exp_out"), sem("top_ready")
        rank_made, slots_ready, experts_ready = sem("rank_made"), sem("slots_ready"), sem("experts_ready")
        table_clear, staged, table_loaded = sem("table_clear"), sem("staged"), sem("table_loaded")
        put_done = two("put_done")
        chunk_loaded = [sem(f"chunk_loaded{i}") for i in range(3)]
        chunk_high, chunk_low = sem("chunk_high"), sem("chunk_low")
        xt_loaded, acc_loaded, acc_store = two("xt_loaded"), two("acc_loaded"), two("acc_store")
        gu_made, silu_ready, h_ready = sem("gu_made"), sem("silu_ready"), sem("h_ready")
        ht_made, ht_high, ht_low, down_made = sem("ht_made"), sem("ht_high"), sem("ht_low"), sem("down_made")
        acc_ready, y_ready = sem("acc_ready"), sem("y_ready")
        xg_loaded, xe_made, xe_high, xe_low, y_store = two("xg_loaded"), sem("xe_made"), sem("xe_high"), sem("xe_low"), two("y_store")
        y_loaded, row_loaded, row_ready, out_store = two("y_loaded"), two("row_loaded"), sem("row_ready"), two("out_store")
        block = ctx.enter_context(nc.Block())

        UA = 2 * TA
        NC = KC + IC
        USES = [len(range(i, NC, 3)) for i in range(3)]

        def unit_of(t, late):
            return 2 * t + (NJ if late else 0)

        def shared_steps(e, late, step):
            first, n = (TA, NT - TA) if late else (0, TA)
            for t in range(first, first + 2):
                step(t, t % 2)
            with e.Fori(0, (n - 4) // 2) as i:
                step(2 * i + first + 2, 0)
                step(2 * i + first + 3, 1)
            for t in range(first + n - 2, first + n):
                step(t, t % 2)

        def inside(t, late, d):
            return not isinstance(t, int) or (TA if late else 0) <= t + d < (NT if late else TA)

        def chunk(x, c):
            if c < KC:
                parts = [w[:, x, c, :] if isinstance(x, int) else w[:, bass.ds(x, 1), c, :].rearrange("p a n -> p (a n)")
                         for w in exu]
                return rows[:, c % 3, :], io["gu_chunk"](x, c), *parts
            i = c - KC
            n = min(P, INT - i * P)
            parts = [w[0:n, x, i, :] if isinstance(x, int) else w[0:n, bass.ds(x, 1), i, :].rearrange("p a n -> p (a n)")
                     for w in exd]
            return rows[0:n, c % 3, 0:DIM], io["down_chunk"](x, i, n), *parts

        @block.sync
        def _(sp):
            for t, name in ((tri, "tri"), (ones, "ones"), (iota, "iota"), (token, "token")):
                sp.dma_start(t[:, :], io[name]).then_inc(consts_in, 16)

            def load_xt(t, k, late):
                if late and isinstance(t, int) and t < TA + 2:
                    sp.wait_ge(gu_made, UA + NJ)
                else:
                    wait(sp, gu_made, unit_of(t, late) - 2)
                sp.dma_start(xt[:, k, :, :], io["xt_row"](t)).then_inc(xt_loaded[k], 16)

            def load_acc(t, k):
                wait(sp, acc_store[k], (t - k) * 8)
                sp.dma_start(acc[:, k, :], io["x1_row"](t)).then_inc(acc_loaded[k], 16)

            def store_acc(t, k):
                sp.wait_ge(acc_ready, t + 1)
                sp.dma_start(io["acc_row"](t), acc[:, k, :]).then_inc(acc_store[k], 16)

            def load_row(m, k):
                sp.wait_ge(acc_store[k], (m - k) * 8 + 16)
                wait(sp, out_store[k], (m - k) * 8)
                sp.dma_start(out_row[:, k, :], io["acc_row"](m)).then_inc(row_loaded[k], 16)

            def store_out(m, k):
                sp.wait_ge(row_ready, m + 1)
                sp.dma_start(io["out_row"](m), out_row[:, k, :]).then_inc(out_store[k], 16)

            load_xt(0, 0, False)
            load_acc(0, 0)

            def early(t, k, x=None):
                if inside(t, False, 1):
                    load_xt(t + 1, 1 - k, False)
                if x is not None:
                    weights(x)
                if inside(t, False, -1):
                    store_acc(t - 1, 1 - k)
                if inside(t, False, 1):
                    load_acc(t + 1, 1 - k)

            def weights(x):
                for c in range(NC):
                    buf, dram, _, _ = chunk(x, c)
                    wait(sp, chunk_low, NC * x + (c - 2 if c else 0))
                    sp.dma_start(buf, dram).then_inc(chunk_loaded[c % 3], 16)

            for t in range(2):
                early(t, t % 2, t)
            with sp.Fori(0, (E - 2) // 2) as i:
                early(2 * i + 2, 0, 2 * i + 2)
                early(2 * i + 3, 1, 2 * i + 3)
            for t in range(E, TA):
                early(t, t % 2)
            store_acc(TA - 1, 1)

            sp.wait_ge(put_done[0], 64 * (NT // 4))
            sp.wait_ge(put_done[1], 64 * (NT // 4))
            sp.dma_start(slot_token[:, :], io["table"]).then_inc(table_loaded, 16)

            def routed(j, k):
                sp.wait_ge(y_ready, j + 1)
                sp.dma_start(io["y_rows"](j), y_out[:, k, :]).then_inc(y_store[k], 16)

            pairs(sp, NJ, 2, routed)
            load_xt(TA, 0, True)
            load_acc(TA, 0)

            def late(t, k):
                if inside(t, True, 1):
                    load_xt(t + 1, 1 - k, True)
                if inside(t, True, -1):
                    if not (isinstance(t, int) and t == TA + 1):
                        store_out(t - TA - 2, k)
                    load_row(t - TA - 1, 1 - k)
                    store_acc(t - 1, 1 - k)
                if inside(t, True, 1):
                    load_acc(t + 1, 1 - k)

            shared_steps(sp, True, late)
            store_acc(NT - 1, 1)
            done = NT - TA - 2
            store_out(done, done % 2)
            for m in range(done + 1, NT):
                load_row(m, m % 2)
                store_out(m, m % 2)
            for s in out_store:
                sp.wait_ge(s, 16 * (NT // 2))

        @block.scalar
        def _(act):
            act.wait_ge(exp_in, 1)
            act.activation(work, work, ACT.Exp).then_inc(exp_out, 1)
            act.wait_ge(exp_in, 2)
            act.activation(small[:, 3, :], small[:, 3, :], ACT.Exp).then_inc(exp_out, 1)

            def silu_of(u, k):
                act.wait_ge(gu_made, u + 1)
                wait(act, h_ready, u - 1)
                act.activation(silu[:, k, :], gu_ps[:, k, 0, 0:INT], ACT.Silu).then_inc(silu_ready, 1)

            def ht_high_of(u, k):
                act.wait_ge(ht_made, u + 1)
                wait(act, down_made, u - 1)
                act.activation(ht[:, k, 0, :], h_ps[:, 0:IP], ACT.Copy).then_inc(ht_high, 1)

            def chunks(x, lo, hi):
                for c in range(lo, hi):
                    buf, _, high, _ = chunk(x, c)
                    act.wait_ge(chunk_loaded[c % 3], 16 * (USES[c % 3] * x + c // 3 + 1))
                    act.activation(high, buf, ACT.Copy).then_inc(chunk_high, 1)

            def shared(t, late, x=None):
                u = unit_of(t, late)
                silu_of(u + 1, 1)
                if x is not None:
                    chunks(x, 0, 2)
                ht_high_of(u, 0)
                if x is not None:
                    chunks(x, 2, 4)
                if inside(t, late, 1):
                    silu_of(u + 2, 0)
                if x is not None:
                    chunks(x, 4, 6)
                ht_high_of(u + 1, 1)
                if x is not None:
                    chunks(x, 6, 7)

            act.wait_ge(pool_zero, 2)
            silu_of(0, 0)
            for t in range(2):
                shared(t, False, t)
            with act.Fori(0, (E - 2) // 2) as i:
                shared(2 * i + 2, False, 2 * i + 2)
                shared(2 * i + 3, False, 2 * i + 3)
            for t in range(E, TA):
                shared(t, False)

            def xe_high_of(j, k):
                act.wait_ge(xe_made, j + 1)
                act.wait_ge(gu_made, UA + j - 1)
                act.activation(xt[:, k, 0, :], x_ps[:, :], ACT.Copy).then_inc(xe_high, 1)

            def y_of(j, k):
                act.wait_ge(down_made, UA + j + 1)
                wait(act, y_store[k], (j - k) * 8)
                act.activation(y_out[:, k, :], y_ps[:, k, :], ACT.Copy).then_inc(y_ready, 1)

            act.wait_ge(chunk_low, NC * E)
            xe_high_of(0, 0)
            xe_high_of(1, 1)
            silu_of(UA, 0)

            def routed(j, k):
                if is_between(j, 0, NJ - 1):
                    silu_of(UA + j + 1, 1 - k)
                ht_high_of(UA + j, k)
                if is_between(j, 0, NJ - 2):
                    xe_high_of(j + 2, k)
                if is_between(j, 1, NJ):
                    y_of(j - 1, 1 - k)

            pairs(act, NJ, 2, routed)
            y_of(NJ - 1, 1)
            silu_of(unit_of(TA, True), 0)
            shared_steps(act, True, lambda t, k: shared(t, True))

        @block.vector
        def _(dve):
            links = [0]

            def link(ins):
                links[0] += 1
                ins.then_inc(chain, 1)
                dve.wait_ge(chain, links[0])

            dve.memset(h[:, :, INT:IP], 0.0).then_inc(h_pad, 1)
            dve.wait_ge(consts_in, 64)
            iota_e = iota[:, 0:E].unsqueeze(1).to_broadcast([P, NT, E])

            def spread(v):
                return v.unsqueeze(2).to_broadcast([P, NT, E])

            def best(scores, peak, top, pick):
                link(dve.tensor_reduce(peak, scores, AX.X, ALU.max))
                link(dve.tensor_tensor(top, scores, spread(peak), ALU.is_ge))
                link(dve.scalar_tensor_tensor(out=top, in0=top, scalar=-float(E), in1=iota_e, op0=ALU.mult, op1=ALU.add))
                link(dve.tensor_reduce(pick, top, AX.X, ALU.min))
                link(dve.tensor_tensor(top, top, spread(pick), ALU.is_equal))

            peak1, peak2, pick, e2, total, p1, p2, den = (small[:, i, :] for i in range(8))
            best(logits[:, :, :], peak1, top1[:, :, :], pick)
            link(dve.scalar_tensor_tensor(out=work, in0=top1[:, :, :], scalar=-3e38, in1=logits[:, :, :],
                                          op0=ALU.mult, op1=ALU.add))
            best(work, peak2, top2[:, :, :], pick)
            dve.tensor_tensor(rank[:, 0, :, :], top1[:, :, :], top2[:, :, :], ALU.add).then_inc(top_ready, 1)
            dve.tensor_tensor(work, logits[:, :, :], spread(peak1), ALU.subtract).then_inc(exp_in, 1)
            dve.tensor_tensor(e2, peak2, peak1, ALU.subtract).then_inc(exp_in, 1)
            dve.wait_ge(exp_out, 2)
            link(dve.tensor_reduce(total, work, AX.X, ALU.add))
            link(dve.reciprocal(p1, total))
            link(dve.tensor_tensor(p2, e2, p1, ALU.mult))
            link(dve.scalar_tensor_tensor(out=den, in0=p1, scalar=1e-20, in1=p2, op0=ALU.add, op1=ALU.add))
            link(dve.reciprocal(den, den))
            link(dve.tensor_scalar(den, den, gates[:, 3:4], None, ALU.mult))
            link(dve.tensor_tensor(weight[:, 0, :], p1, den, ALU.mult))
            link(dve.tensor_tensor(weight[:, 1, :], p2, den, ALU.mult))
            dve.wait_ge(rank_made, 1)
            link(dve.tensor_copy(rank, x_ps[:, :].rearrange("p (a t e) -> p a t e", a=2, e=E)))
            for x in range(E):
                ins = dve.tensor_tensor_scan(before[:, :, x], ones[:, 0:NT], rank[:, 1, :, x], 0.0, ALU.mult, ALU.add)
            link(ins)
            count, padded, upto, base = tiles[:, 0, :], tiles[:, 1, :], tiles[:, 2, :], tiles[:, 3, :]
            link(dve.tensor_scalar(tiles_i[:, 0, :], before[:, NT - 1, :], float(P - 1), None, ALU.add))
            link(dve.tensor_scalar(tiles_i[:, 1, :], tiles_i[:, 0, :], 7, None, ALU.logical_shift_right))
            link(dve.tensor_copy(padded, tiles_i[:, 1, :]))
            link(dve.tensor_tensor_scan(upto, ones[:, 0:E], padded, 0.0, ALU.mult, ALU.add))
            link(dve.tensor_tensor(base, upto, padded, ALU.subtract))
            link(dve.tensor_scalar(base, base, float(P), None, ALU.mult))
            link(dve.tensor_tensor(before, before, rank[:, 1, :, :], ALU.subtract))
            link(dve.tensor_tensor(before, before, rank[:, 0, :, :], ALU.add))
            link(dve.tensor_tensor(before, before, base.unsqueeze(1).to_broadcast([P, NT, E]), ALU.add))
            for r, top in enumerate((top1, top2)):
                link(dve.tensor_tensor(work, before, top[:, :, :], ALU.mult))
                link(dve.tensor_reduce(slot_f[:, 0, r, :], work, AX.X, ALU.add))
            link(dve.tensor_copy(slot[:, :, :], slot_f[:, 0, :, :]))
            link(dve.tensor_scalar(slot_part[:, 0, :, :], slot[:, :, :], P - 1, None, ALU.bitwise_and))
            link(dve.tensor_scalar(slot_part[:, 1, :, :], slot[:, :, :], 7, None, ALU.logical_shift_right))
            link(dve.tensor_copy(slot_f[:, :, :, :], slot_part[:, :, :, :]))
            dve.scalar_tensor_tensor(out=table_at[:, :, :], in0=slot_f[:, 0, :, :], scalar=float(NJ),
                                     in1=slot_f[:, 1, :, :], op0=ALU.mult, op1=ALU.add).then_inc(slots_ready, 1)
            link(dve.tensor_scalar(experts_f[:, :], iota[0:1, E:E + NJ], tiles[0:1, 2, 0:1], None, ALU.is_ge))
            for x in range(1, E):
                link(dve.scalar_tensor_tensor(out=experts_f[:, :], in0=iota[0:1, E:E + NJ], scalar=tiles[0:1, 2, x:x + 1],
                                              in1=experts_f[:, :], op0=ALU.is_ge, op1=ALU.add))
            dve.tensor_scalar(experts[:, :], experts_f[:, :], float(E - 1), None, ALU.min).then_inc(experts_ready, 1)

            def h_of(u, k):
                dve.wait_ge(silu_ready, u + 1)
                wait(dve, ht_made, u - 1)
                dve.tensor_tensor(h[:, k, 0:INT], silu[:, k, :], gu_ps[:, k, 1, 0:INT], ALU.mult).then_inc(h_ready, 1)

            def ht_low_of(u, k):
                dve.wait_ge(ht_high, u + 1)
                dve.tensor_tensor(ht[:, k, 1, :], h_ps[:, 0:IP], ht[:, k, 0, :], ALU.subtract).then_inc(ht_low, 1)

            def acc_of(t, k, late):
                dve.wait_ge(down_made, unit_of(t, late) + 2)
                dve.wait_ge(acc_loaded[k], (t - k) * 8 + 16)
                dve.scalar_tensor_tensor(out=acc[:, k, :], in0=y_ps[:, k, :], scalar=gates[:, 3:4], in1=acc[:, k, :],
                                         op0=ALU.mult, op1=ALU.add).then_inc(acc_ready, 1)

            def chunks(x, lo, hi):
                for c in range(lo, hi):
                    buf, _, high, low = chunk(x, c)
                    dve.wait_ge(chunk_high, NC * x + c + 1)
                    dve.tensor_tensor(low, buf, high, ALU.subtract).then_inc(chunk_low, 1)

            def column(m):
                return slice(m, m + 1) if isinstance(m, int) else bass.ds(m, 1)

            def combine(m, k):
                dve.wait_ge(row_loaded[k], (m - k) * 8 + 16)
                dve.wait_ge(y_loaded[k], (m - k) * 16 + 32)
                row = out_row[:, k, :]
                dve.scalar_tensor_tensor(out=row, in0=y_in[:, k, 0, :], scalar=weight[:, 0, column(m)], in1=row,
                                         op0=ALU.mult, op1=ALU.add).then_inc(chain, 1)
                dve.wait_ge(chain, links[0] + m + 1)
                dve.scalar_tensor_tensor(out=row, in0=y_in[:, k, 1, :], scalar=weight[:, 1, column(m)], in1=row,
                                         op0=ALU.mult, op1=ALU.add).then_inc(row_ready, 1)

            def shared(t, k, late, x=None):
                u = unit_of(t, late)
                h_of(u + 1, 1)
                if x is not None:
                    chunks(x, 0, 2)
                ht_low_of(u, 0)
                if x is not None:
                    chunks(x, 2, 4)
                if inside(t, late, -1):
                    acc_of(t - 1, 1 - k, late)
                if inside(t, late, 1):
                    h_of(u + 2, 0)
                if x is not None:
                    chunks(x, 4, 6)
                ht_low_of(u + 1, 1)
                if x is not None:
                    chunks(x, 6, 7)
                if late and inside(t, late, -1):
                    combine(t - TA - 1, 1 - k)

            h_of(0, 0)
            for t in range(2):
                shared(t, t % 2, False, t)
            with dve.Fori(0, (E - 2) // 2) as i:
                shared(2 * i + 2, 0, False, 2 * i + 2)
                shared(2 * i + 3, 1, False, 2 * i + 3)
            for t in range(E, TA):
                shared(t, t % 2, False)
            acc_of(TA - 1, 1, False)

            def xe_low_of(j, k):
                dve.wait_ge(xe_high, j + 1)
                dve.tensor_tensor(xt[:, k, 1, :], x_ps[:, :], xt[:, k, 0, :], ALU.subtract).then_inc(xe_low, 1)

            xe_low_of(0, 0)
            xe_low_of(1, 1)
            h_of(UA, 0)

            def routed(j, k):
                if is_between(j, 0, NJ - 1):
                    h_of(UA + j + 1, 1 - k)
                ht_low_of(UA + j, k)
                if is_between(j, 0, NJ - 2):
                    xe_low_of(j + 2, k)

            pairs(dve, NJ, 2, routed)
            h_of(unit_of(TA, True), 0)
            shared_steps(dve, True, lambda t, k: shared(t, k, True))
            acc_of(NT - 1, 1, True)
            for m in range(NT - TA - 1, NT):
                combine(m, m % 2)

        @block.gpsimd
        def _(pool):
            pool.memset(exd[0][:, :, IC - 1, :], 0.0).then_inc(pool_zero, 1)
            pool.memset(exd[1][:, :, IC - 1, :], 0.0).then_inc(pool_zero, 1)
            pool.memset(slot_token[:, :], 0).then_inc(pool_zero, 1)
            pool.wait_ge(pool_zero, 3)
            pool.dma_start(io["table"], slot_token[:, :]).then_inc(table_clear, 16)
            pool.wait_ge(table_clear, 16)
            pool.wait_ge(slots_ready, 1)

            def put(i, k):
                wait(pool, put_done[k], 64 * ((i - k) // 2) if isinstance(i, int) else (i - k) * 32)
                two_tiles = slice(2 * i, 2 * i + 2) if isinstance(i, int) else bass.ds(2 * i, 2)
                pool.tensor_copy(put_at[:, k, :, :], table_at[:, :, two_tiles]).then_inc(staged, 1)
                pool.tensor_copy(put_token[:, k, :], token[:, two_tiles]).then_inc(staged, 1)
                wait_alone(pool, staged, 2 * i + 2, passed)
                for r in range(2):
                    for q in range(2):
                        pool.indirect_dma_start(io["table_cells"], bass.IndirectOffsetOnAxis(ap=put_at[:, k, r, q:q + 1], axis=0),
                                                put_token[:, k, q:q + 1], None).then_inc(put_done[k], 16)

            pairs(pool, NT // 2, 2, put)

            def fetch(j, k):
                wait(pool, xe_made, j - 1)
                pool.tensor_copy(get_at[:, k, 0:1], slot_token[:, j:j + 1] if isinstance(j, int)
                                 else slot_token[:, bass.ds(j, 1)]).then_inc(staged, 1)
                wait_alone(pool, staged, NT + j + 1, passed)
                pool.indirect_dma_start(xg[:, k, :], None, io["xn_rows"],
                                        bass.IndirectOffsetOnAxis(ap=get_at[:, k, 0:1], axis=0)).then_inc(xg_loaded[k], 16)

            pool.wait_ge(table_loaded, 16)
            pool.wait_ge(chunk_low, NC * E)
            pairs(pool, NJ, 2, fetch)
            for s in y_store:
                pool.wait_ge(s, 8 * NJ)

            def collect(m, k):
                wait(pool, row_ready, m - 1)
                pool.tensor_copy(get_at[:, k, :], slot[:, :, m] if isinstance(m, int)
                                 else slot[:, :, bass.ds(m, 1)].rearrange("p r a -> p (r a)")).then_inc(staged, 1)
                wait_alone(pool, staged, NT + NJ + m + 1, passed)
                for r in range(2):
                    pool.indirect_dma_start(y_in[:, k, r, :], None, io["y_all"],
                                            bass.IndirectOffsetOnAxis(ap=get_at[:, k, r:r + 1], axis=0)).then_inc(y_loaded[k], 16)

            pairs(pool, NT, 2, collect)

        @block.tensor
        def _(pe):
            PARTS = ((0, 0), (0, 1), (1, 0))

            def up(u, k, slot_k, wu):
                wait(pe, h_ready, u - 1)
                for c in range(KC):
                    for n, (a, w) in enumerate(PARTS):
                        for side in range(2):
                            mm = pe.matmul(gu_ps[:, k, side, 0:INT], xt[:, slot_k, a, c * P:(c + 1) * P], wu(w, c, side),
                                           start=(c == 0 and n == 0), stop=(c == KC - 1 and n == 2))
                mm.then_inc(gu_made, 1)

            def turn_h(u, k):
                pe.wait_ge(h_ready, u + 1)
                wait(pe, ht_low, u)
                for c in range(IC):
                    mm = pe.transpose(h_ps[:, c * P:(c + 1) * P], h[:, k, c * P:(c + 1) * P], ident[:, :])
                mm.then_inc(ht_made, 1)

            def down(u, k, yk, wd, start, stop):
                pe.wait_ge(ht_high, u + 1)
                pe.wait_ge(ht_low, u + 1)
                for c in range(IC):
                    for n, (a, w) in enumerate(PARTS):
                        mm = pe.matmul(y_ps[:, yk, :], ht[:, k, a, c * P:(c + 1) * P], wd(w, c),
                                       start=(start and c == 0 and n == 0), stop=(stop and c == IC - 1 and n == 2))
                mm.then_inc(down_made, 1)

            def up_shared(i):
                return lambda w, c, side: shu[w][:, i, c, side * INT:(side + 1) * INT]

            def down_shared(i):
                return lambda w, c: shd[w][:, i, c, :]

            def shared(t, k, late):
                u = unit_of(t, late)
                up(u + 1, 1, k, up_shared(1))
                turn_h(u, 0)
                if inside(t, late, -1):
                    down(u - 1, 1, 1 - k, down_shared(1), False, True)
                if inside(t, late, 1):
                    pe.wait_ge(xt_loaded[1 - k], (t + 1 - (1 - k)) * 8 + 16)
                    up(u + 2, 0, 1 - k, up_shared(0))
                turn_h(u + 1, 1)
                if late and isinstance(t, int) and t < TA + 2:
                    pe.wait_ge(y_ready, NJ)
                else:
                    wait(pe, acc_ready, t - 1)
                down(u, 0, k, down_shared(0), True, False)

            pe.wait_ge(h_pad, 1)
            pe.wait_ge(consts_in, 64)
            pe.wait_ge(xt_loaded[0], 16)
            up(0, 0, 0, up_shared(0))
            pe.wait_ge(top_ready, 1)
            chosen = rank[:, 0, :, :].rearrange("p t e -> p (t e)")
            pe.matmul(x_ps[:, 0:NT * E], tri[:, :], chosen, start=True, stop=True)
            pe.matmul(x_ps[:, NT * E:2 * NT * E], ones[:, :], chosen, start=True, stop=True).then_inc(rank_made, 1)
            shared_steps(pe, False, lambda t, k: shared(t, k, False))
            down(UA - 1, 1, 1, down_shared(1), False, True)

            def turn_x(j, k):
                pe.wait_ge(xg_loaded[k], (j - k) * 8 + 16)
                wait(pe, xe_low, j)
                for c in range(KC):
                    mm = pe.transpose(x_ps[:, c * P:(c + 1) * P], xg[:, k, c * P:(c + 1) * P], ident[:, :])
                mm.then_inc(xe_made, 1)

            def expert(j):
                at = slice(j, j + 1) if isinstance(j, int) else bass.ds(j, 1)
                return pe.value_load(experts[0:1, at], min_val=0, max_val=E - 1)

            def up_routed(j, k):
                r = expert(j)
                pe.wait_ge(xe_low, j + 1)
                up(UA + j, k, k, lambda w, c, side: exu[w][:, bass.ds(r, 1), c, side * INT:(side + 1) * INT].rearrange("p a n -> p (a n)"))

            def down_routed(j, k):
                r = expert(j)
                if isinstance(j, int) and j < 2:
                    pe.wait_ge(acc_ready, TA)
                else:
                    pe.wait_ge(y_ready, j - 1)
                down(UA + j, k, k, lambda w, c: exd[w][:, bass.ds(r, 1), c, :].rearrange("p a n -> p (a n)"), True, True)

            pe.wait_ge(experts_ready, 1)
            pe.wait_ge(pool_zero, 2)
            pe.wait_ge(chunk_low, NC * E)
            turn_x(0, 0)
            turn_x(1, 1)
            up_routed(0, 0)

            def routed(j, k):
                if is_between(j, 0, NJ - 1):
                    up_routed(j + 1, 1 - k)
                turn_h(UA + j, k)
                if is_between(j, 0, NJ - 2):
                    turn_x(j + 2, k)
                if is_between(j, 1, NJ):
                    down_routed(j - 1, 1 - k)

            pairs(pe, NJ, 2, routed)
            down_routed(NJ - 1, 1)
            pe.wait_ge(xt_loaded[0], 16 * (TA // 2 + 1))
            up(unit_of(TA, True), 0, 0, up_shared(0))
            shared_steps(pe, True, lambda t, k: shared(t, k, True))
            down(unit_of(NT, True) - 1, 1, 1, down_shared(1), False, True)


def build(nc, a, out):
    x_tiles = a["x"].rearrange("b (q p) c -> p b q c", p=P)
    scratch = {n: nc.dram_tensor(n, shape, dt).ap() for n, shape, dt in (
        ("gate_s", (P, B, 2, DIM), F32), ("x1_s", (NT, P, DIM), F32), ("xn_s", (NT * P, DIM), F32),
        ("xt_s", (NT, P, 2, DIM), BF16), ("acc_s", (NT, P, DIM), F32), ("y_s", (NJ * P, DIM), F32),
        ("table_s", (P * NJ, 1), I32))}
    out_tiles = out.rearrange("b (q p) c -> (b q) p c", p=P)
    ctx_rows = a["ctx"].rearrange("b (q p) c -> p b q c", p=P)

    def pick(ap, i, how):
        if isinstance(i, int):
            return ap[i]
        return ap[bass.ds(i, 1)].rearrange(how)

    def batch(ap, b):
        if isinstance(b, int):
            return ap[:, b, :, :]
        return ap[:, bass.ds(b, 1), :, :].rearrange("p a q c -> p (a q) c")

    ctx_t = a["ctx_t"].rearrange("b h d s -> d b h s")
    io = {
        "wht": a["wht"], "ident": a["ident"], "gates": a["gates"], "wg": a["wg"], "decay": a["decay"],
        "wh": a["wh"], "wo": a["wo"], "wr": a["wr"], "affine": a["affine"], "tri": a["tri"], "ones": a["ones"],
        "iota": a["iota"], "token": a["token"], "gu": a["gu"], "down": a["down"],
        "x_batch": lambda b: batch(x_tiles, b),
        "c_batch": lambda b: batch(ctx_rows, b),
        "ct_batch": lambda b: batch(ctx_t, b),
        "gate_tile": lambda b, q: scratch["gate_s"][:, b, q, :] if isinstance(b, int)
        else scratch["gate_s"][:, bass.ds(b, 1), q, :].rearrange("p a c -> p (a c)"),
        "gate_batch": lambda b: batch(scratch["gate_s"], b),
        "x1_tile": lambda b, q: pick(scratch["x1_s"], 2 * b + q, "a p c -> (a p) c"),
        "xn_tile": lambda b, q: pick(scratch["xn_s"].rearrange("(t p) c -> t p c", p=P), 2 * b + q, "a p c -> (a p) c"),
        "xt_tile": lambda b, q: pick(scratch["xt_s"], 2 * b + q, "a p r c -> (a p) r c"),
        "xt_row": lambda t: pick(scratch["xt_s"], t, "a p r c -> (a p) r c"),
        "x1_row": lambda t: pick(scratch["x1_s"], t, "a p c -> (a p) c"),
        "acc_row": lambda t: pick(scratch["acc_s"], t, "a p c -> (a p) c"),
        "out_row": lambda t: pick(out_tiles, t, "a p c -> (a p) c"),
        "y_rows": lambda j: pick(scratch["y_s"].rearrange("(j p) c -> j p c", p=P), j, "a p c -> (a p) c"),
        "y_all": scratch["y_s"], "xn_rows": scratch["xn_s"],
        "table": scratch["table_s"].rearrange("(p j) o -> p (j o)", p=P), "table_cells": scratch["table_s"],
        "gu_chunk": lambda x, c: pick(a["gu"], x, "a p c n -> (a p) c n")[:, c, :],
        "down_chunk": lambda x, i, n: pick(a["down"], x, "a i c -> (a i) c")[i * P:i * P + n, :],
    }
    with ExitStack() as ctx:
        def sb(name, shape, dt):
            return ctx.enter_context(nc.sbuf_tensor(name, shape, dt))

        keep = {
            "ident": sb("ident", [P, P], F32), "gates": sb("gates", [P, 4], F32), "logits": sb("logits", [P, NT, E], F32),
            "shu_hi": sb("shu_hi", [P, 2, KC, 2 * INT], BF16), "shu_lo": sb("shu_lo", [P, 2, KC, 2 * INT], BF16),
            "shd_hi": sb("shd_hi", [P, 2, IC, DIM], BF16), "shd_lo": sb("shd_lo", [P, 2, IC, DIM], BF16)}
        keep["gu_sh_chunks"] = lambda pool, stage, loaded, link: shared_weights(pool, io, keep, stage, loaded, link)
        with ExitStack() as two:
            for n in ("at_hi", "at_lo"):
                keep[n] = two.enter_context(nc.sbuf_tensor(n, [P, H, 2, S], F32R))
            scores_stage(nc, io, keep)
            mix_stage(nc, io, keep)
        ffn_stage(nc, io, keep)


def shape_constants():
    gam = (1.0 - 2.0 ** (-5.0 - np.arange(H, dtype=np.float32))).astype(np.float32)
    idx = np.arange(S, dtype=np.float32)
    expo = idx[None, :] - idx[:, None]
    d = np.where(expo[None] <= 0, gam[:, None, None] ** expo[None], 0.0).astype(np.float32)
    d = d / np.sqrt(d.sum(axis=-1))[:, None, :] / np.float32(np.sqrt(HD))
    dt = d.transpose(2, 0, 1)
    decay = np.concatenate([dt[0:P, 0:2].reshape(P, -1), dt[0:P, 2:4].reshape(P, -1), dt[P:S, :, P:S].reshape(P, -1)], 1)
    iota = np.concatenate([np.arange(E), np.arange(NJ)])
    return {
        "ident": np.eye(P, dtype=np.float32), "tri": np.triu(np.ones((P, P), np.float32), 1),
        "ones": np.ones((P, P), np.float32), "decay": decay.reshape(P, 3, DIM).astype(np.float32),
        "iota": np.broadcast_to(iota.astype(np.float32), (P, E + NJ)),
        "token": (np.arange(NT)[None, :] * P + np.arange(P)[:, None]).astype(np.int32)}


def kernel(x, ctx_2048, g_xattn, g_ffn, L0_xattn_Wh, L0_xattn_wg_w, L0_xattn_wo_w, L0_xattn_gn_gamma,
           L0_xattn_gn_beta, L0_ffn_gate_w, L0_ffn_expert_gate, L0_ffn_expert_up, L0_ffn_expert_down,
           L0_ffn_shared_gate, L0_ffn_shared_up, L0_ffn_shared_down):
    import concourse.bacc as bacc
    from concourse.bass_utils import run_bass_kernel_spmd

    def rows(w, n=DIM):
        return np.asarray(w).reshape(-1, P, n).transpose(1, 0, 2)

    ctx = np.asarray(ctx_2048)
    wh = np.asarray(L0_xattn_Wh)
    gate = np.concatenate([np.asarray(L0_ffn_expert_gate), np.asarray(L0_ffn_shared_gate).reshape(2, INT, DIM)])
    up = np.concatenate([np.asarray(L0_ffn_expert_up), np.asarray(L0_ffn_shared_up).reshape(2, INT, DIM)])
    gu = np.concatenate([gate, up], 1).transpose(0, 2, 1).reshape(NB, KC, P, 2 * INT).transpose(0, 2, 1, 3)
    down = np.concatenate([np.asarray(L0_ffn_expert_down).transpose(0, 2, 1),
                           np.asarray(L0_ffn_shared_down).T.reshape(2, INT, DIM)])
    arrays = {
        "x": np.asarray(x), "ctx": ctx, "ctx_t": ctx.reshape(B, S, H, HD).transpose(0, 2, 3, 1),
        "gates": np.broadcast_to(np.concatenate([np.asarray(g_xattn), np.asarray(g_ffn)]), (P, 2)),
        "wht": wh.transpose(2, 0, 1), "wh": wh.transpose(1, 0, 2), "wg": rows(L0_xattn_wg_w), "wo": rows(L0_xattn_wo_w),
        "wr": rows(np.asarray(L0_ffn_gate_w).T, E),
        "affine": np.broadcast_to(np.stack([np.asarray(L0_xattn_gn_gamma), np.asarray(L0_xattn_gn_beta)]), (P, 2, DIM)),
        "gu": gu, "down": down, **shape_constants()}
    arrays = {n: np.ascontiguousarray(v) for n, v in arrays.items()}
    nc = bacc.Bacc("TRN2", target_bir_lowering=False, num_devices=1)
    aps = {n: nc.dram_tensor(n + "_dram", v.shape, mybir.dt.from_np(v.dtype), kind="ExternalInput").ap()
           for n, v in arrays.items()}
    out = nc.dram_tensor("out_dram", (B, S, DIM), F32, kind="ExternalOutput").ap()
    build(nc, aps, out)
    r = run_bass_kernel_spmd(nc, [{n + "_dram": v for n, v in arrays.items()}], core_ids=[0])
    return r.results[0]["out_dram"]
```

```python
import numpy as np
import concourse.bass as bass
from concourse import mybir
from contextlib import ExitStack

F32, F32R, BF16, I32 = mybir.dt.float32, mybir.dt.float32r, mybir.dt.bfloat16, mybir.dt.int32
ALU = mybir.AluOpType
ACT = mybir.ActivationFunctionType
AX = mybir.AxisListType

P = 128
B, S, DIM = 16, 256, 512
H, HD = 4, 128
NT = B * S // P
KC = DIM // P
E, INT = 8, 352
NB = E + 2
IP = 384
IC = IP // P
NJ = (2 * B * S + E * (P - 1)) // P
EF = 2
NC = KC + IC
TA = 2 * (E - EF)
PAD = INT - (IC - 1) * P
LN_EPS, GN_EPS = 1e-5, 1e-3


def wait(e, sem, count):
    if isinstance(count, int) and count <= 0:
        return
    e.wait_ge(sem, count)


def wait_alone(e, sem, count, passed):
    wait(e, sem, count)
    e.sem_inc(passed, 1)


def pairs(e, n, peel, step):
    for t in range(peel):
        step(t, t % 2)
    with e.Fori(0, (n - 2 * peel) // 2) as i:
        step(2 * i + peel, 0)
        step(2 * i + peel + 1, 1)
    for t in range(n - peel - n % 2, n):
        step(t, t % 2)


def is_between(t, lo, hi):
    return not isinstance(t, int) or lo <= t < hi


EXW = 2 * (KC * 2 * INT + IC * DIM)


def part_start(p, c):
    if c < KC:
        return (p * KC + c) * 2 * INT
    if c < NC - 1:
        return 2 * KC * 2 * INT + (p * (IC - 1) + c - KC) * DIM
    return EXW - (2 - p) * DIM


def chunk_shape(c):
    return (P, 2 * INT) if c < KC else (min(P, INT - (c - KC) * P), DIM)


def chunk_in_dram(io, x, c):
    return io["gu_chunk"](x, c) if c < KC else io["down_chunk"](x, c - KC, chunk_shape(c)[0])


def scores_stage(nc, io, keep):
    ctx = ExitStack()
    with ctx:
        def sb(name, shape, dt):
            return ctx.enter_context(nc.sbuf_tensor(name, shape, dt))

        def pb(name, shape):
            return ctx.enter_context(nc.psum_tensor(name, shape, F32))

        def sem(name):
            return ctx.enter_context(nc.semaphore(name))

        ident, at_hi, at_lo, gates = keep["ident"], keep["at_hi"], keep["at_lo"], keep["gates"]
        x_in = sb("x_in", [P, 2, 2, DIM], F32)
        xn = sb("xn", [P, 2, 2, DIM], F32)
        xt_hi = sb("xt_hi", [P, 2, 2, KC, P], F32R)
        xt_lo = sb("xt_lo", [P, 2, 2, KC, P], F32R)
        ct_in = sb("ct_in", [P, 2, H, S], F32)
        ct_hi = sb("ct_hi", [P, 2, H, S], F32R)
        ct_lo = sb("ct_lo", [P, 2, H, S], F32R)
        q_hi = sb("q_hi", [P, H, S], F32R)
        q_lo = sb("q_lo", [P, H, S], F32R)
        w_out = keep["w_out"]
        wg_hi = sb("wg_hi", [P, KC, DIM], F32R)
        wg_lo = sb("wg_lo", [P, KC, DIM], F32R)
        g_hi = sb("g_hi", [P, H, HD], F32R)
        g_lo = sb("g_lo", [P, H, HD], F32R)
        wht = sb("wht", [P, H, HD], F32)
        zeros = sb("zeros", [P, DIM], BF16)
        stats = sb("stats", [P, 2, 2, 6], F32)
        mv = sb("mv", [P, 2, 2, 2], F32)
        sd = sb("sd", [P, 2, 2], F32)
        rstd = sb("rstd", [P, 2, 2], F32)
        eps = sb("eps", [P, 1], F32)
        warm = sb("warm", [P, 1], F32)
        decay = sb("decay", [P, 3, DIM], F32)
        wg_in = sb("wg_in", [P, KC, DIM], F32)
        masked = wg_in
        stage = sb("stage", [P, 2, 2 * INT], F32)
        parts = sb("parts", [P, 2, 2, 2 * INT], BF16)

        s_ps = pb("s_ps", [P, 3, DIM])
        t_ps = pb("t_ps", [P, 2, DIM])
        q_ps = pb("q_ps", [P, 2, DIM])
        w_ps = pb("w_ps", [P, DIM])

        consts_in, wg_loaded, decay_loaded = sem("consts_in"), sem("wg_loaded"), sem("decay_loaded")
        x_loaded = [sem("x_loaded0"), sem("x_loaded1")]
        ct_loaded = [sem("ct_loaded0"), sem("ct_loaded1")]
        gate_store = keep["gate_store"]
        g_made, g_high, g_split = sem("g_made"), sem("g_high"), sem("g_split")
        wg_high, wg_split, eps_set, zero_set = sem("wg_high"), sem("wg_split"), sem("eps_set"), sem("zero_set")
        chain, var_ready, sd_ready, xn_ready = sem("chain"), sem("var_ready"), sem("sd_ready"), sem("xn_ready")
        xt_made, xt_high, xt_low = sem("xt_made"), sem("xt_high"), sem("xt_low")
        q_made, q_high, q_low = sem("q_made"), sem("q_high"), sem("q_low")
        ct_high, ct_low = sem("ct_high"), sem("ct_low")
        gate_made, gate_relu, s_added = sem("gate_made"), sem("gate_relu"), sem("s_added")
        a_ready, a_high, upper_set = sem("a_ready"), sem("a_high"), sem("upper_set")
        gates_loaded, wht_loaded, warmed, s_abs = sem("gates_loaded"), sem("wht_loaded"), sem("warmed"), sem("s_abs")
        a_split, mix_loaded, mix_high = sem("a_split"), sem("mix_loaded"), sem("mix_high")
        stage_loaded = [sem("stage_loaded0"), sem("stage_loaded1")]
        parts_store = [sem("parts_store0"), sem("parts_store1")]
        pool_chain, tanh_done, passed = sem("pool_chain"), sem("tanh_done"), sem("passed")
        block = ctx.enter_context(nc.Block())

        def bank(t, i):
            return t[:, i, :]

        def a_part(t, i):
            return t[:, 2 * i:2 * i + 2, 0, :] if i < 2 else t[:, :, 1, P:S]

        def masked_part(i):
            return masked[:, i, :].rearrange("p (h s) -> p h s", h=2 if i < 2 else H)

        @block.sync
        def _(sp):
            sp.dma_start(wht[:, :, :], io["wht"]).then_inc(wht_loaded, 16)
            sp.dma_start(x_in[:, 0, :, :], io["x_batch"](0)).then_inc(x_loaded[0], 16)
            sp.dma_start(ident[:, :], io["ident"]).then_inc(consts_in, 16)
            sp.dma_start(wg_in[:, :, :], io["wg"]).then_inc(wg_loaded, 16)

            def step(b, k):
                if not (isinstance(b, int) and b == 0):
                    wait(sp, xn_ready, b - 1)
                    sp.dma_start(x_in[:, k, :, :], io["x_batch"](b)).then_inc(x_loaded[k], 16)
                wait(sp, ct_low, b - 1)
                sp.dma_start(ct_in[:, k, :, :], io["ct_batch"](b)).then_inc(ct_loaded[k], 16)
                if isinstance(b, int) and b == 0:
                    sp.dma_start(gates[:, 0:2], io["gates"]).then_inc(gates_loaded, 16)
                if isinstance(b, int) and b == 1:
                    sp.dma_start(decay[:, :, :], io["decay"]).then_inc(decay_loaded, 16)
                    sp.dma_start(keep["wh"][:, :, :], io["wh"]).then_inc(mix_loaded, 16)
                    for n in range(2):
                        sp.dma_start(keep["c_in"][:, n, :, :], io["c_batch"](n)).then_inc(mix_loaded, 16)

            pairs(sp, B, 2, step)

        @block.scalar
        def _(act):
            act.wait_ge(eps_set, 1)
            act.activation(warm[:, :], eps[:, :], ACT.Sqrt).then_inc(warmed, 1)

            def root(b, k):
                act.wait_ge(var_ready, b + 1)
                act.activation(sd[:, k, :], mv[:, k, :, 1], ACT.Sqrt, bias=eps[:, 0:1]).then_inc(sd_ready, 1)

            def xt_high_part(b, k):
                for q in range(2):
                    act.wait_ge(xt_made, 2 * b + q + 1)
                    wait(act, gate_made, 2 * b - 2)
                    act.activation(xt_hi[:, k, q, :, :], bank(t_ps, q).rearrange("p (k t) -> p k t", k=KC),
                                   ACT.Copy).then_inc(xt_high, 1)

            def ct_high_part(b, k):
                act.wait_ge(ct_loaded[k], 16 * (b // 2) + 16 if isinstance(b, int) else (b - k) * 8 + 16)
                wait(act, s_added, b - 1)
                act.activation(ct_hi[:, k, :, :], ct_in[:, k, :, :], ACT.Copy).then_inc(ct_high, 1)

            def gate_out(b, q):
                act.wait_ge(gate_made, 2 * b + q + 1)
                wait(act, gate_store[q], 16 * b)
                act.activation(w_out[:, q, :], w_ps[:, :], ACT.Relu).then_inc(gate_relu, 1)
                act.wait_ge(gate_relu, 2 * b + q + 1)
                act.dma_start(io["gate_tile"](b, q), w_out[:, q, :]).then_inc(gate_store[q], 16)

            root(0, 0)
            act.wait_ge(g_made, 1)
            act.activation(g_hi[:, :, :], bank(q_ps, 0).rearrange("p (h d) -> p h d", h=H), ACT.Copy).then_inc(g_high, 1)
            xt_high_part(0, 0)
            root(1, 1)
            act.wait_ge(wg_loaded, 16)
            act.activation(wg_hi[:, :, :], wg_in[:, :, :], ACT.Copy).then_inc(wg_high, 1)
            ct_high_part(0, 0)

            def step(b, k):
                if isinstance(b, int) and b == B - 2:
                    act.wait_ge(mix_loaded, 48)
                    for n in ("wh", "c_in"):
                        high = keep[{"wh": "wh_hi", "c_in": "c_hi"}[n]]
                        flat = [t[:, :, :] if n == "wh" else t[:, :, :, :] for t in (high, keep[n])]
                        act.activation(flat[0], flat[1], ACT.Copy).then_inc(mix_high, 1)
                for i in range(2):
                    act.wait_ge(q_made, 2 * b + i + 1)
                    wait(act, s_added, b)
                    act.activation(q_hi[:, 2 * i:2 * i + 2, :], bank(q_ps, i).rearrange("p (h s) -> p h s", h=2),
                                   ACT.Copy).then_inc(q_high, 1)
                if is_between(b, 0, B - 1):
                    xt_high_part(b + 1, 1 - k)
                    ct_high_part(b + 1, 1 - k)
                if is_between(b, 0, B - 2):
                    root(b + 2, k)
                if isinstance(b, int) and b == B - 1:
                    gate_out(B - 2, 1)
                else:
                    gate_out(b, 0)
                if not isinstance(b, int) or b < B - 2:
                    gate_out(b, 1)

            pairs(act, B, 2, step)
            act.wait_ge(gates_loaded, 16)
            act.activation(gates[:, 2:4], gates[:, 0:2], ACT.Tanh).then_inc(tanh_done, 1)
            act.wait_ge(s_added, B)
            for i in range(3):
                act.activation(masked[:, i, :], bank(s_ps, i), ACT.Abs).then_inc(s_abs, 1)
            gate_out(B - 1, 0)
            for i in range(3):
                act.wait_ge(a_ready, i + 1)
                act.activation(a_part(at_hi, i), masked_part(i), ACT.Copy).then_inc(a_high, 1)
            gate_out(B - 1, 1)

        @block.vector
        def _(dve):
            links = [0]

            def link(ins):
                links[0] += 1
                ins.then_inc(chain, 1)
                dve.wait_ge(chain, links[0])

            dve.memset(eps[:, :], LN_EPS).then_inc(eps_set, 1)
            dve.memset(zeros[:, :], 0.0).then_inc(zero_set, 1)

            def moments(b, k, n):
                dve.wait_ge(x_loaded[k], (b - k) * 8 + 16)
                for q in range(2):
                    ins = dve.bn_stats(stats[:, k, q, :], x_in[:, k, q, :])
                ins.then_inc(chain, 1)
                wait_alone(dve, chain, n + 1, passed)
                for q in range(2):
                    ins = dve.bn_aggr(mv[:, k, q, :], stats[:, k, q, :])
                ins.then_inc(var_ready, 1)

            def normalise(b, k, n):
                dve.wait_ge(sd_ready, b + 1)
                dve.reciprocal(rstd[:, k, :], sd[:, k, :]).then_inc(chain, 1)
                dve.wait_ge(chain, n + 2)
                wait(dve, xt_made, 2 * b - 2)
                for q in range(2):
                    ins = dve.tensor_scalar(xn[:, k, q, :], x_in[:, k, q, :], mv[:, k, q, 0:1],
                                            rstd[:, k, q:q + 1], ALU.subtract, ALU.mult)
                ins.then_inc(xn_ready, 1)

            def xt_low_part(b, k):
                for q in range(2):
                    dve.wait_ge(xt_high, 2 * b + q + 1)
                    dve.tensor_tensor(xt_lo[:, k, q, :, :], bank(t_ps, q).rearrange("p (k t) -> p k t", k=KC),
                                      xt_hi[:, k, q, :, :].bitcast(F32), ALU.subtract).then_inc(xt_low, 1)

            def ct_low_part(b, k):
                dve.wait_ge(ct_high, b + 1)
                dve.tensor_tensor(ct_lo[:, k, :, :], ct_in[:, k, :, :], ct_hi[:, k, :, :].bitcast(F32),
                                  ALU.subtract).then_inc(ct_low, 1)

            moments(0, 0, 0)
            normalise(0, 0, 0)
            dve.wait_ge(g_high, 1)
            dve.tensor_tensor(g_lo[:, :, :], bank(q_ps, 0).rearrange("p (h d) -> p h d", h=H),
                              g_hi[:, :, :].bitcast(F32), ALU.subtract).then_inc(g_split, 1)
            xt_low_part(0, 0)
            moments(1, 1, 2)
            normalise(1, 1, 2)
            dve.wait_ge(wg_high, 1)
            dve.tensor_tensor(wg_lo[:, :, :], wg_in[:, :, :], wg_hi[:, :, :].bitcast(F32),
                              ALU.subtract).then_inc(wg_split, 1)
            ct_low_part(0, 0)

            def step(b, k):
                at_start = isinstance(b, int) and b == 0
                if is_between(b, 0, B - 2) and not at_start:
                    moments(b + 2, k, 2 * b + 4)
                for i in range(2):
                    dve.wait_ge(q_high, 2 * b + i + 1)
                    dve.tensor_tensor(q_lo[:, 2 * i:2 * i + 2, :], bank(q_ps, i).rearrange("p (h s) -> p h s", h=2),
                                      q_hi[:, 2 * i:2 * i + 2, :].bitcast(F32), ALU.subtract).then_inc(q_low, 1)
                if is_between(b, 0, B - 1):
                    xt_low_part(b + 1, 1 - k)
                    ct_low_part(b + 1, 1 - k)
                if at_start:
                    moments(b + 2, k, 2 * b + 4)
                if is_between(b, 0, B - 2):
                    normalise(b + 2, k, 2 * b + 4)
                if isinstance(b, int) and b == B - 2:
                    dve.wait_ge(mix_high, 2)
                    dve.tensor_tensor(keep["wh_lo"][:, :, :], keep["wh"][:, :, :], keep["wh_hi"][:, :, :].bitcast(F32),
                                      ALU.subtract)
                    for n in range(2):
                        dve.tensor_tensor(keep["c_lo"][:, n, :, :], keep["c_in"][:, n, :, :],
                                          keep["c_hi"][:, n, :, :].bitcast(F32), ALU.subtract)

            pairs(dve, B, 2, step)
            links[0] = 2 * B
            dve.wait_ge(decay_loaded, 16)
            for i in range(3):
                m = masked[:, i, :]
                dve.wait_ge(s_abs, i + 1)
                link(dve.tensor_tensor(m, m, decay[:, i, :], ALU.mult))
                dve.tensor_scalar(m, m, 1.0, None, ALU.max).then_inc(a_ready, 1)
            for i in range(3):
                dve.wait_ge(a_high, i + 1)
                dve.tensor_tensor(a_part(at_lo, i), masked_part(i), a_part(at_hi, i).bitcast(F32),
                                  ALU.subtract).then_inc(a_split, 1)

        @block.gpsimd
        def _(pool):
            links = [0]

            def link(ins):
                links[0] += 1
                ins.then_inc(pool_chain, 1)
                pool.wait_ge(pool_chain, links[0])

            pool.memset(at_hi[:, :, 1, 0:P].bitcast(F32), 1.0).then_inc(upper_set, 1)
            pool.memset(at_lo[:, :, 1, 0:P].bitcast(F32), 0.0).then_inc(upper_set, 1)
            shared_weights(pool, io, keep, stage, parts, stage_loaded, parts_store, link)

        @block.tensor
        def _(pe):
            pe.wait_ge(wht_loaded, 16)
            for h in range(H):
                mm = pe.matmul(q_ps[:, 0, h * HD:(h + 1) * HD], wht[:, h, :], wht[:, h, :], start=True, stop=True)
            mm.then_inc(g_made, 1)
            pe.wait_ge(zero_set, 1)
            for i in range(3):
                pe.matmul(bank(s_ps, i), zeros[:, 0:P], zeros[:, :], start=True, stop=False, skip_group_check=True)

            def turn(b, k):
                pe.wait_ge(xn_ready, b + 1)
                for q in range(2):
                    wait(pe, xt_low, 2 * b + q - 1)
                    for c in range(KC):
                        mm = pe.transpose(t_ps[:, q, c * P:(c + 1) * P], xn[:, k, q, c * P:(c + 1) * P], ident[:, :])
                    mm.then_inc(xt_made, 1)

            def gate(b, k, q):
                wait(pe, gate_relu, 2 * b + q)
                for c in range(KC):
                    for n, (a, w) in enumerate(((xt_hi, wg_hi), (xt_hi, wg_lo), (xt_lo, wg_hi))):
                        mm = pe.matmul(w_ps[:, :], a[:, k, q, c, :], w[:, c, :], start=(c == 0 and n == 0),
                                       stop=(c == KC - 1 and n == 2))
                mm.then_inc(gate_made, 1)

            pe.wait_ge(consts_in, 16)
            turn(0, 0)
            pe.wait_ge(g_split, 1)

            def step(b, k):
                pe.wait_ge(xt_high, 2 * b + 2)
                pe.wait_ge(xt_low, 2 * b + 2)
                for i in range(2):
                    wait(pe, q_low, 2 * b + i - 1)
                    for h in (2 * i, 2 * i + 1):
                        out = q_ps[:, i, (h % 2) * S:(h % 2 + 1) * S]
                        for n, (g, a) in enumerate(((g_hi, xt_hi), (g_hi, xt_lo), (g_lo, xt_hi))):
                            mm = pe.matmul(out, g[:, h, :], a[:, k, :, h, :], start=(n == 0), stop=(n == 2))
                    mm.then_inc(q_made, 1)
                if is_between(b, 0, B - 1):
                    turn(b + 1, 1 - k)
                if isinstance(b, int) and b == 0:
                    pe.wait_ge(wg_split, 1)
                if isinstance(b, int) and b == B - 1:
                    gate(B - 2, 1 - k, 1)
                else:
                    gate(b, k, 0)
                pe.wait_ge(q_high, 2 * b + 2)
                pe.wait_ge(q_low, 2 * b + 2)
                pe.wait_ge(ct_high, b + 1)
                pe.wait_ge(ct_low, b + 1)
                for h in range(H):
                    for kt in range(2):
                        out = s_ps[:, h // 2, (h % 2) * S:(h % 2 + 1) * S] if kt == 0 else s_ps[:, 2, h * P:(h + 1) * P]
                        for c, a in ((ct_hi, q_hi), (ct_hi, q_lo), (ct_lo, q_hi)):
                            mm = pe.matmul(out, c[:, k, h, kt * P:(kt + 1) * P], a[:, h, kt * P:S], start=False,
                                           stop=False, skip_group_check=True)
                mm.then_inc(s_added, 1)
                if isinstance(b, int) and b == B - 1:
                    gate(b, k, 0)
                if not (isinstance(b, int) and b == B - 2):
                    gate(b, k, 1)

            pairs(pe, B, 2, step)


def shared_weights(pool, io, keep, stage, parts, stage_loaded, parts_store, link):
    wu, wd = (keep["shu_hi"], keep["shu_lo"]), (keep["shd_hi"], keep["shd_lo"])
    for w in wd:
        link(pool.memset(w[:, :, IC - 1, :], 0.0))

    def source(n):
        blk, c = n // NC, n % NC
        rows, width = chunk_shape(c)
        return stage[0:rows, n % 2, 0:width], chunk_in_dram(io, E + blk if blk < 2 else blk - 2, c)

    def load(n):
        s, dram = source(n)
        pool.dma_start(s, dram).then_inc(stage_loaded[n % 2], 16)

    total = (2 + EF) * NC
    load(0)
    load(1)
    for n in range(total):
        blk, c = n // NC, n % NC
        rows, width = chunk_shape(c)
        s, _ = source(n)
        if blk < 2:
            hi, lo = (w[0:rows, blk, c, :] if c < KC else w[0:rows, blk, c - KC, :] for w in (wu if c < KC else wd))
        else:
            hi, lo = (parts[0:rows, n % 2, p, 0:width] for p in range(2))
            wait(pool, parts_store[n % 2], 16 * ((n - 2 * NC) // 2))
        pool.wait_ge(stage_loaded[n % 2], 16 * (n // 2 + 1))
        link(pool.tensor_scalar(hi, s, 1.0, None, ALU.mult))
        link(pool.tensor_tensor(lo, s, hi, ALU.subtract))
        if n + 2 < total:
            load(n + 2)
        if blk >= 2:
            pool.dma_start(io["first_parts"](blk - 2, c), parts[0:rows, n % 2, :, 0:width]).then_inc(parts_store[n % 2], 16)
    for k in range(2):
        pool.wait_ge(parts_store[k], 16 * len(range(k, EF * NC, 2)))


def mix_stage(nc, io, keep):
    ctx = ExitStack()
    with ctx:
        def sb(name, shape, dt):
            return ctx.enter_context(nc.sbuf_tensor(name, shape, dt))

        def pb(name, shape):
            return ctx.enter_context(nc.psum_tensor(name, shape, F32))

        def sem(name):
            return ctx.enter_context(nc.semaphore(name))

        ident, at_hi, at_lo, gates, logits = (keep[n] for n in ("ident", "at_hi", "at_lo", "gates", "logits"))
        x_in = sb("x2_in", [P, 2, 2, DIM], F32)
        w_in = sb("w_in", [P, 2, 2, DIM], F32)
        u_hi = sb("u_hi", [P, H, S], F32R)
        u_lo = sb("u_lo", [P, H, S], F32R)
        nrm = sb("nrm", [P, 2, DIM], F32)
        z = sb("z", [P, 2, 2, DIM], F32)
        zt_hi = sb("zt_hi", [P, 2, KC, P], F32R)
        zt_lo = sb("zt_lo", [P, 2, KC, P], F32R)
        x1 = sb("x1", [P, 2, DIM], F32)
        xn = sb("xn2", [P, 2, DIM], F32)
        xt = sb("xt_f", [P, 2, DIM], F32)
        xt16 = sb("xt16", [P, 2, 2, DIM], BF16)
        c_in, c_hi, c_lo, wh_hi, wh_lo = (keep[n] for n in ("c_in", "c_hi", "c_lo", "wh_hi", "wh_lo"))
        wo = sb("wo", [P, KC, DIM], F32)
        wo_hi = sb("wo_hi", [P, KC, DIM], F32R)
        wo_lo = sb("wo_lo", [P, KC, DIM], F32R)
        wr = sb("wr", [P, KC, E], F32)
        affine = sb("affine", [P, 2, DIM], F32)
        o_stats = sb("o_stats", [P, 2, 6], F32)
        o_mv = sb("o_mv", [P, 2, 2], F32)
        o_sd = sb("o_sd", [P, 2], F32)
        o_rstd = sb("o_rstd", [P, 2, 2], F32)
        x_stats = sb("x_stats", [P, 2, 6], F32)
        x_mv = sb("x_mv", [P, 2, 2], F32)
        x_sd = sb("x_sd", [P, 2], F32)
        x_rstd = sb("x_rstd", [P, 2, 2], F32)
        eps = sb("eps2", [P, 2], F32)

        u_ps = pb("u_ps", [P, 2, DIM])
        o_ps = pb("o_ps", [P, 2, DIM])
        t_ps = pb("t2_ps", [P, 2, DIM])
        y_ps = pb("y_ps", [P, 2, DIM])

        def two(name):
            return [sem(name + "0"), sem(name + "1")]

        wo_in = sem("wo_in")
        consts_in, weights_high, weights_split, eps_set = (
            sem("consts2_in"), sem("weights_high"), sem("weights_split"), sem("eps2_set"))
        c_loaded, x_loaded, w_loaded = two("c_loaded"), two("x2_loaded"), two("w_loaded")
        c_high, c_low, u_made, u_high, u_low = (sem("c_high"), sem("c_low"), sem("u_made"), sem("u_high"), sem("u_low"))
        o_made, o_var, o_root, o_scale, n_ready, z_ready = (
            sem("o_made"), sem("o_var"), sem("o_root"), sem("o_scale"), sem("n_ready"), sem("z_ready"))
        zt_made, zt_high, zt_low, y_made, x1_ready = (
            sem("zt_made"), sem("zt_high"), sem("zt_low"), sem("y_made"), sem("x1_ready"))
        x_var, x_root, x_scale, xn_ready = sem("x_var"), sem("x_root"), sem("x_scale"), sem("xn2_ready")
        xt_made, xt_copied, xt_high, xt_low = sem("xt2_made"), sem("xt_copied"), sem("xt2_high"), sem("xt2_low")
        r_made, r_kept, chain, pool_chain = sem("r_made"), sem("r_kept"), sem("chain2"), sem("pool_chain2")
        passed = sem("passed2")
        x1_store, xn_store, xt_store = (keep[n] for n in ("x1_store", "xn_store", "xt_store"))
        block = ctx.enter_context(nc.Block())

        def batches(e, step):
            for b in range(4):
                step(b, b % 2)
            with e.Fori(0, (B - 6) // 2) as i:
                step(2 * i + 4, 0)
                step(2 * i + 5, 1)
            for b in range(B - 2, B + 2):
                step(b, b % 2)

        @block.sync
        def _(sp):
            sp.dma_start(wo[:, :, :], io["wo"]).then_inc(wo_in, 16)
            sp.dma_start(wr[:, :, :], io["wr"]).then_inc(consts_in, 16)
            sp.dma_start(affine[:, :, :], io["affine"]).then_inc(consts_in, 16)
            for n in ("tri", "ones", "iota", "token"):
                sp.dma_start(keep[n][:, :], io[n]).then_inc(consts_in, 16)
            for q in range(2):
                sp.wait_ge(keep["gate_store"][q], 16 * B)
            sp.dma_start(w_in[:, 0, :, :], io["gate_batch"](0)).then_inc(w_loaded[0], 16)

            def stores(b, q):
                sp.wait_ge(xn_ready, 2 * b + q + 1)
                sp.dma_start(io["x1_tile"](b, q), x1[:, q, :]).then_inc(x1_store[q], 16)
                sp.dma_start(io["xn_tile"](b, q), xn[:, q, :]).then_inc(xn_store[q], 16)

            def step(b, k):
                if is_between(b, 0, B - 1):
                    wait(sp, z_ready, 2 * b)
                    sp.dma_start(w_in[:, 1 - k, :, :], io["gate_batch"](b + 1)).then_inc(w_loaded[1 - k], 16)
                if is_between(b, 0, B):
                    wait(sp, x1_ready, 2 * b - 2)
                    sp.dma_start(x_in[:, k, :, :], io["x_batch"](b)).then_inc(x_loaded[k], 16)
                if is_between(b, 0, B - 2):
                    wait(sp, c_low, b - 1)
                    sp.dma_start(c_in[:, k, :, :], io["c_batch"](b + 2)).then_inc(c_loaded[k], 16)
                if isinstance(b, int) and b == B:
                    sp.wait_ge(xt_store[0], 16 * (B - 3))
                    sp.dma_start(keep["xt_parts"][:, 0, :, :], io["xt_row"](0)).then_inc(keep["xt_loaded"][0], 16)
                if is_between(b - 2, 0, B):
                    stores(b - 2, 1)
                    for q in range(2):
                        sp.wait_ge(xt_low, 2 * (b - 2) + q + 1)
                        sp.dma_start(io["xt_tile"](b - 2, q), xt16[:, q, :, :]).then_inc(xt_store[q], 16)
                if is_between(b - 1, 0, B):
                    stores(b - 1, 0)

            batches(sp, step)

        @block.scalar
        def _(act):
            act.wait_ge(eps_set, 2)

            def c_high_part(b, k):
                act.wait_ge(c_loaded[k], (b - k) * 8)
                wait(act, u_made, 2 * b - 2)
                act.activation(c_hi[:, k, :, :], c_in[:, k, :, :], ACT.Copy).then_inc(c_high, 1)

            def u_high_part(b):
                for i in range(2):
                    act.wait_ge(u_made, 2 * b + i + 1)
                    wait(act, o_made, 2 * b)
                    act.activation(u_hi[:, 2 * i:2 * i + 2, :], u_ps[:, i, :].rearrange("p (h s) -> p h s", h=2),
                                   ACT.Copy).then_inc(u_high, 1)

            def norm_o(b, q):
                act.wait_ge(o_var, 2 * b + q + 1)
                act.activation(o_sd[:, q:q + 1], o_mv[:, q, 1:2], ACT.Sqrt, bias=eps[:, 1:2]).then_inc(o_root, 1)
                act.wait_ge(o_scale, 2 * b + q + 1)
                wait(act, z_ready, 2 * b + q - 1)
                act.activation(nrm[:, q, :], o_ps[:, q, :], ACT.Identity, bias=o_rstd[:, q, 1:2],
                               scale=o_rstd[:, q, 0:1]).then_inc(n_ready, 1)

            def norm_x(b, q):
                act.wait_ge(x_var, 2 * b + q + 1)
                act.activation(x_sd[:, q:q + 1], x_mv[:, q, 1:2], ACT.Sqrt, bias=eps[:, 0:1]).then_inc(x_root, 1)
                act.wait_ge(x_scale, 2 * b + q + 1)
                wait(act, xt_made, 2 * b + q - 1)
                wait(act, xn_store[q], 16 * b)
                act.activation(xn[:, q, :], x1[:, q, :], ACT.Identity, bias=x_rstd[:, q, 1:2],
                               scale=x_rstd[:, q, 0:1]).then_inc(xn_ready, 1)

            u_high_part(0)

            def step(b, k):
                if is_between(b - 2, 0, B):
                    norm_x(b - 2, 1)
                if is_between(b, 0, B):
                    norm_o(b, 0)
                    norm_o(b, 1)
                if is_between(b - 1, 0, B):
                    for q in range(2):
                        act.wait_ge(zt_made, 2 * (b - 1) + q + 1)
                        wait(act, y_made, 2 * (b - 2) + q + 1)
                        act.activation(zt_hi[:, q, :, :], y_ps[:, q, :].rearrange("p (k t) -> p k t", k=KC),
                                       ACT.Copy).then_inc(zt_high, 1)
                if is_between(b, 0, B - 1):
                    u_high_part(b + 1)
                if is_between(b - 2, 0, B):
                    for q in range(2):
                        act.wait_ge(xt_made, 2 * (b - 2) + q + 1)
                        wait(act, xt_low, 2 * (b - 2) + q - 1)
                        act.activation(xt[:, q, :], t_ps[:, q, :], ACT.Copy).then_inc(xt_copied, 1)
                if is_between(b - 2, 0, B):
                    for q in range(2):
                        act.wait_ge(xt_copied, 2 * (b - 2) + q + 1)
                        wait(act, xt_store[q], 16 * (b - 2))
                        act.activation(xt16[:, q, 0, :], xt[:, q, :], ACT.Copy).then_inc(xt_high, 1)
                if isinstance(b, int) and b == 0:
                    act.wait_ge(wo_in, 16)
                    act.activation(wo_hi[:, :, :], wo[:, :, :], ACT.Copy).then_inc(weights_high, 1)
                if is_between(b, 0, B - 2):
                    c_high_part(b + 2, k)
                if is_between(b - 1, 0, B):
                    norm_x(b - 1, 0)

            batches(act, step)

        @block.vector
        def _(dve):
            dve.memset(eps[:, 0:1], LN_EPS).then_inc(eps_set, 1)
            dve.memset(eps[:, 1:2], GN_EPS).then_inc(eps_set, 1)
            LINKS = 2

            def norm(src, stats, mv, sd, rstd, var, root, scale, n, i, q):
                dve.bn_stats(stats[:, q, :], src).then_inc(chain, 1)
                wait_alone(dve, chain, n + 1, passed)
                dve.bn_aggr(mv[:, q, :], stats[:, q, :]).then_inc(var, 1)
                dve.wait_ge(root, i + 1)
                dve.reciprocal(rstd[:, q, 0:1], sd[:, q:q + 1]).then_inc(chain, 1)
                dve.wait_ge(chain, n + LINKS)
                dve.scalar_tensor_tensor(out=rstd[:, q, 1:2], in0=mv[:, q, 0:1], scalar=-1.0, in1=rstd[:, q, 0:1],
                                         op0=ALU.mult, op1=ALU.mult).then_inc(scale, 1)

            def norm_o(b, q, n):
                dve.wait_ge(o_made, 2 * b + q + 1)
                norm(o_ps[:, q, :], o_stats, o_mv, o_sd, o_rstd, o_var, o_root, o_scale, n, 2 * b + q, q)

            def residual(b, q, n):
                dve.wait_ge(y_made, 2 * b + q + 1)
                dve.wait_ge(x_loaded[kof(b, q)], xcount(b))
                wait(dve, x1_store[q], 16 * b)
                wait(dve, xn_ready, 2 * b + q - 1)
                dve.scalar_tensor_tensor(out=x1[:, q, :], in0=y_ps[:, q, :], scalar=gates[:, 2:3],
                                         in1=x_in[:, kof(b, q), q, :], op0=ALU.mult,
                                         op1=ALU.add).then_inc(x1_ready, 1)
                dve.wait_ge(x1_ready, 2 * b + q + 1)
                norm(x1[:, q, :], x_stats, x_mv, x_sd, x_rstd, x_var, x_root, x_scale, n, 2 * b + q, q)

            parity = [0]

            def kof(b, q):
                return parity[0]

            def xcount(b):
                return (b - parity[0]) * 8 + 16

            def u_low_part(b):
                for i in range(2):
                    dve.wait_ge(u_high, 2 * b + i + 1)
                    dve.tensor_tensor(u_lo[:, 2 * i:2 * i + 2, :], u_ps[:, i, :].rearrange("p (h s) -> p h s", h=2),
                                      u_hi[:, 2 * i:2 * i + 2, :].bitcast(F32), ALU.subtract).then_inc(u_low, 1)

            u_low_part(0)

            def step(b, k):
                if is_between(b - 2, 0, B):
                    parity[0] = k
                    residual(b - 2, 1, LINKS * links_before(b, 0))
                if is_between(b, 0, B):
                    norm_o(b, 0, LINKS * links_before(b, 1))
                    norm_o(b, 1, LINKS * links_before(b, 2))
                if is_between(b - 3, 0, B):
                    keep_logits(b - 3)
                if is_between(b - 1, 0, B):
                    for q in range(2):
                        dve.wait_ge(zt_high, 2 * (b - 1) + q + 1)
                        dve.tensor_tensor(zt_lo[:, q, :, :], y_ps[:, q, :].rearrange("p (k t) -> p k t", k=KC),
                                          zt_hi[:, q, :, :].bitcast(F32), ALU.subtract).then_inc(zt_low, 1)
                if is_between(b, 0, B - 1):
                    u_low_part(b + 1)
                if is_between(b - 2, 0, B):
                    for q in range(2):
                        dve.wait_ge(xt_high, 2 * (b - 2) + q + 1)
                        dve.tensor_tensor(xt16[:, q, 1, :], xt[:, q, :], xt16[:, q, 0, :],
                                          ALU.subtract).then_inc(xt_low, 1)
                if isinstance(b, int) and b == 0:
                    dve.wait_ge(weights_high, 1)
                    dve.tensor_tensor(wo_lo[:, :, :], wo[:, :, :], wo_hi[:, :, :].bitcast(F32),
                                      ALU.subtract).then_inc(weights_split, 1)
                if is_between(b - 1, 0, B):
                    parity[0] = 1 - k
                    residual(b - 1, 0, LINKS * links_before(b, 3))

            def keep_logits(b):
                for q in range(2):
                    dve.wait_ge(r_made, 2 * b + q + 1)
                    dve.tensor_copy(logits_of(b, q), t_ps[:, q, 0:E]).then_inc(r_kept, 1)

            def logits_of(b, q):
                t = 2 * b + q
                return logits[:, t, :] if isinstance(t, int) else logits[:, bass.ds(t, 1), :].rearrange("p a e -> p (a e)")

            def links_before(b, part):
                if not isinstance(b, int):
                    return 4 * b - 3 + part
                done = 0
                for s in range(b + 1):
                    for i, there in enumerate((0 <= s - 2 < B, s < B, s < B, 0 <= s - 1 < B)):
                        if s == b and i == part:
                            return done
                        done += there
                return done

            batches(dve, step)
            keep_logits(B - 1)

        @block.gpsimd
        def _(pool):
            def c_low_part(b, k):
                pool.wait_ge(c_high, b - 1)
                pool.tensor_tensor(c_lo[:, k, :, :], c_in[:, k, :, :], c_hi[:, k, :, :].bitcast(F32),
                                   ALU.subtract).then_inc(c_low, 1)

            pool.wait_ge(consts_in, 96)

            def step(b, k):
                if is_between(b, 0, B):
                    for q in range(2):
                        i = 2 * b + q
                        pool.wait_ge(n_ready, i + 1)
                        pool.tensor_tensor(nrm[:, q, :], nrm[:, q, :], affine[:, 0, :], ALU.mult).then_inc(pool_chain, 1)
                        pool.wait_ge(pool_chain, 2 * i + 1)
                        pool.tensor_tensor(nrm[:, q, :], nrm[:, q, :], affine[:, 1, :], ALU.add).then_inc(pool_chain, 1)
                        pool.wait_ge(pool_chain, 2 * i + 2)
                        pool.wait_ge(w_loaded[k], (b - k) * 8 + 16)
                        wait(pool, zt_made, i - 3)
                        pool.tensor_tensor(z[:, k, q, :], nrm[:, q, :], w_in[:, k, q, :], ALU.mult).then_inc(z_ready, 1)
                if is_between(b, 0, B - 2):
                    c_low_part(b + 2, k)

            batches(pool, step)

        @block.tensor
        def _(pe):
            def attend(b, k):
                wait(pe, c_high, b - 1)
                wait(pe, c_low, b - 1)
                for i in range(2):
                    wait(pe, u_low, 2 * b + i - 1)
                    for h in (2 * i, 2 * i + 1):
                        n = 0
                        for kt in range(2):
                            for c, a in ((c_hi, at_hi), (c_hi, at_lo), (c_lo, at_hi)):
                                mm = pe.matmul(u_ps[:, i, (h % 2) * S:(h % 2 + 1) * S], c[:, k, kt, h * HD:(h + 1) * HD],
                                               a[:, h, kt, :], start=(n == 0), stop=(n == 5))
                                n += 1
                    mm.then_inc(u_made, 1)

            attend(0, 0)

            def step(b, k):
                if is_between(b, 0, B):
                    pe.wait_ge(u_high, 2 * b + 2)
                    pe.wait_ge(u_low, 2 * b + 2)
                    for q in range(2):
                        wait(pe, n_ready, 2 * b + q - 1)
                        for h in range(H):
                            for n, (a, w) in enumerate(((u_hi, wh_hi), (u_hi, wh_lo), (u_lo, wh_hi))):
                                mm = pe.matmul(o_ps[:, q, h * HD:(h + 1) * HD], a[:, h, q * P:(q + 1) * P], w[:, h, :],
                                               start=(n == 0), stop=(n == 2))
                        mm.then_inc(o_made, 1)
                if is_between(b - 1, 0, B):
                    for q in range(2):
                        pe.wait_ge(z_ready, 2 * (b - 1) + q + 1)
                        wait(pe, x1_ready, 2 * (b - 2) + q + 1)
                        for c in range(KC):
                            mm = pe.transpose(y_ps[:, q, c * P:(c + 1) * P], z[:, 1 - k, q, c * P:(c + 1) * P], ident[:, :])
                        mm.then_inc(zt_made, 1)
                if is_between(b, 0, B - 1):
                    attend(b + 1, 1 - k)
                if is_between(b - 2, 0, B):
                    for q in range(2):
                        pe.wait_ge(xn_ready, 2 * (b - 2) + q + 1)
                        wait(pe, r_kept, 2 * (b - 3) + q + 1)
                        for c in range(KC):
                            mm = pe.transpose(t_ps[:, q, c * P:(c + 1) * P], xn[:, q, c * P:(c + 1) * P], ident[:, :])
                        mm.then_inc(xt_made, 1)
                if isinstance(b, int) and b == 1:
                    pe.wait_ge(weights_split, 1)
                if is_between(b - 1, 0, B):
                    for q in range(2):
                        pe.wait_ge(zt_low, 2 * (b - 1) + q + 1)
                        pe.wait_ge(zt_high, 2 * (b - 1) + q + 1)
                        for c in range(KC):
                            for n, (a, w) in enumerate(((zt_hi, wo_hi), (zt_hi, wo_lo), (zt_lo, wo_hi))):
                                mm = pe.matmul(y_ps[:, q, :], a[:, q, c, :], w[:, c, :], start=(c == 0 and n == 0),
                                               stop=(c == KC - 1 and n == 2))
                        mm.then_inc(y_made, 1)
                if isinstance(b, int) and b == 2:
                    pe.wait_ge(consts_in, 96)
                if is_between(b - 2, 0, B):
                    for q in range(2):
                        pe.wait_ge(xt_copied, 2 * (b - 2) + q + 1)
                        for c in range(KC):
                            mm = pe.matmul(t_ps[:, q, 0:E], xt[:, q, c * P:(c + 1) * P], wr[:, c, :], start=(c == 0),
                                           stop=(c == KC - 1))
                        mm.then_inc(r_made, 1)

            batches(pe, step)


def ffn_stage(nc, io, keep):
    ctx = ExitStack()
    with ctx:
        def sb(name, shape, dt):
            return ctx.enter_context(nc.sbuf_tensor(name, shape, dt))

        def pb(name, shape):
            return ctx.enter_context(nc.psum_tensor(name, shape, F32))

        def sem(name):
            return ctx.enter_context(nc.semaphore(name))

        def two(name):
            return [sem(name + "0"), sem(name + "1")]

        ident, gates, logits = keep["ident"], keep["gates"], keep["logits"]
        shu = (keep["shu_hi"], keep["shu_lo"])
        shd = (keep["shd_hi"], keep["shd_lo"])
        ex = sb("ex", [P, E, EXW], BF16)
        xt, tri, ones, iota, token = (keep[n] for n in ("xt_parts", "tri", "ones", "iota", "token"))
        silu = sb("silu", [P, 2, INT], F32)
        h = sb("h", [P, 2, IP], F32)
        ht = sb("ht_parts", [P, 2, 2, IP], BF16)
        rows = sb("rows", [P, 3, 2 * INT], F32)
        acc = sb("acc", [P, 2, DIM], F32)
        pool_row = sb("pool_row", [P, 2, DIM], F32)
        top1, top2 = sb("top1", [P, NT, E], F32), sb("top2", [P, NT, E], F32)
        small = sb("small", [P, 8, NT], F32)
        tiles = sb("tiles", [P, 5, E], F32)
        tiles_i = sb("tiles_i", [P, 2, E], I32)
        weight = sb("weight", [P, 2, NT], F32)
        slot = sb("slot", [P, 2, NT], I32)
        slot_part = sb("slot_part", [P, 2, 2, NT], I32)
        table_at = sb("table_at", [P, 2, NT], I32)
        experts_f = sb("experts_f", [1, NJ], F32)
        experts = sb("experts", [1, NJ], I32)
        slot_token = sb("slot_token", [P, NJ], I32)
        put_at = sb("put_at", [P, 2, 2, 2], I32)
        put_token = sb("put_token", [P, 2, 2], I32)
        get_at = sb("get_at", [P, 3, 2], I32)

        flat = rows[:, :, :].rearrange("p a b -> p (a b)")
        y_out = flat[:, 0:2 * DIM].rearrange("p (a b) -> p a b", a=2)
        rank = pool_row[:, 0, :].rearrange("p (a t e) -> p a t e", a=2, e=E)
        before = pool_row[:, 1, 0:NT * E].rearrange("p (t e) -> p t e", e=E)
        work = pool_row[:, 1, NT * E:2 * NT * E].rearrange("p (t e) -> p t e", e=E)
        xg = pool_row
        y_in = ex[:, 0, 0:12 * DIM].bitcast(F32).rearrange("p (a r b) -> p a r b", a=3, r=2)
        row_in = ex[:, 1, 0:6 * DIM].bitcast(F32).rearrange("p (a b) -> p a b", a=3)
        out_row = ex[:, 1, 6 * DIM:12 * DIM].bitcast(F32).rearrange("p (a b) -> p a b", a=3)

        slot_f = small[:, 0:4, :].rearrange("p (a r) t -> p a r t", a=2)

        gu_ps = pb("gu_ps", [P, 2, 2, DIM])
        h_ps = pb("h_ps", [P, DIM])
        x_ps = pb("x_ps", [P, DIM])
        y_ps = pb("y3_ps", [P, 2, DIM])

        h_pad, passed = sem("h_pad"), sem("passed3")
        pool_zero, first_loaded = sem("pool_zero"), sem("first_loaded")
        chain, exp_in, exp_out, top_ready = sem("chain3"), sem("exp_in"), sem("exp_out"), sem("top_ready")
        rank_made, slots_ready, experts_ready = sem("rank_made"), sem("slots_ready"), sem("experts_ready")
        table_clear, staged, table_loaded = sem("table_clear"), sem("staged"), sem("table_loaded")
        put_done = two("put_done")
        chunk_loaded = [sem(f"chunk_loaded{i}") for i in range(3)]
        chunk_high, chunk_low = sem("chunk_high"), sem("chunk_low")
        xt_loaded, acc_loaded, acc_store = keep["xt_loaded"], two("acc_loaded"), two("acc_store")
        gu_made, silu_ready, h_ready = sem("gu_made"), sem("silu_ready"), sem("h_ready")
        ht_made, ht_high, ht_low, down_made = sem("ht_made"), sem("ht_high"), sem("ht_low"), sem("down_made")
        acc_ready, y_ready = sem("acc_ready"), sem("y_ready")
        xg_loaded, xe_made, xe_high, xe_low, y_store = two("xg_loaded"), sem("xe_made"), sem("xe_high"), sem("xe_low"), two("y_store")
        y_loaded, row_loaded, out_store = ([sem(f"{n}{k}") for k in range(3)] for n in ("y_loaded", "row_loaded", "out_store"))
        row_ready = sem("row_ready")
        block = ctx.enter_context(nc.Block())

        UA = 2 * TA
        USES = [len(range(i, NC, 3)) for i in range(3)]

        def unit_of(t, late):
            return 2 * t + (NJ if late else 0)

        def buffers_of(late):
            return (NJ % 2, 1 - NJ % 2) if late else (0, 1)

        def shared_steps(e, late, step):
            first, n = (TA, NT - TA) if late else (0, TA)
            for t in range(first, first + 2):
                step(t, t % 2)
            with e.Fori(0, (n - 4) // 2) as i:
                step(2 * i + first + 2, 0)
                step(2 * i + first + 3, 1)
            for t in range(first + n - 2, first + n):
                step(t, t % 2)

        def late_pairs(e, pair):
            n = (NT - TA) // 2
            for i in range(3):
                pair(i)
            with e.Fori(0, n - 4) as i:
                pair(i + 3)
            pair(n - 1)

        def combined(i):
            if isinstance(i, int) and i < 3:
                even, odd = (([], [0, 1]), ([2], [3, 4]), ([5, 6], [7, 8]))[i]
                return [[(m, m % 3, m // 3) for m in part] for part in (even, odd)]
            return [(3 * i, 0, i)], [(3 * i + 1, 1, i), (3 * i + 2, 2, i)]

        CUTS = (((0, 1), (1, 2), (2, 3), (3, 4)), ((4, 5), (5, 7), (7, 7), (7, 7)))

        def inside(t, late, d):
            return not isinstance(t, int) or (TA if late else 0) <= t + d < (NT if late else TA)

        def chunk(y, c):
            x = y + EF
            n, width = chunk_shape(c)
            halves = [ex[0:n, x, part_start(p, c):part_start(p, c) + width] if isinstance(x, int) else
                      ex[0:n, bass.ds(x, 1), part_start(p, c):part_start(p, c) + width].rearrange("p a n -> p (a n)")
                      for p in range(2)]
            return rows[0:n, c % 3, 0:width], chunk_in_dram(io, x, c), *halves

        @block.sync
        def _(sp):
            def load_xt(t, k, late):
                if late and isinstance(t, int) and t < TA + 2:
                    sp.wait_ge(gu_made, UA + NJ - (NJ - 1 - k) % 2)
                else:
                    wait(sp, gu_made, unit_of(t, late) - 2)
                sp.dma_start(xt[:, k, :, :], io["xt_row"](t)).then_inc(xt_loaded[k], 16)

            def load_acc(t, k):
                wait(sp, acc_store[k], (t - k) * 8)
                sp.dma_start(acc[:, k, :], io["x1_row"](t)).then_inc(acc_loaded[k], 16)

            def store_acc(t, k):
                sp.wait_ge(acc_ready, t + 1)
                sp.dma_start(io["acc_row"](t), acc[:, k, :]).then_inc(acc_store[k], 16)

            def load_row(m, k):
                wait(sp, row_ready, m - 2)
                sp.dma_start(row_in[:, k, :], io["acc_row"](m)).then_inc(row_loaded[k], 16)

            def store_out(m, k):
                sp.wait_ge(row_ready, m + 1)
                sp.dma_start(io["out_row"](m), out_row[:, k, :]).then_inc(out_store[k], 16)

            def load_chunk(y, c):
                buf, dram, _, _ = chunk(y, c)
                wait(sp, chunk_low, NC * y + (c - 2 if c > 2 else 0))
                sp.dma_start(buf, dram).then_inc(chunk_loaded[c % 3], 16)

            for s in keep["x1_store"] + keep["xn_store"] + keep["xt_store"]:
                sp.wait_ge(s, 16 * B)
            for c in range(3):
                load_chunk(0, c)
            load_xt(1, 1, False)
            load_acc(0, 0)

            def early(t, k, y):
                load_chunk(y, 6 if k else 3)
                if inside(t, False, -1):
                    store_acc(t - 1, 1 - k)
                if inside(t, False, 2):
                    load_xt(t + 2, k, False)
                if inside(t, False, 1):
                    load_acc(t + 1, 1 - k)
                    for c in (0, 1, 2) if k else (4, 5):
                        load_chunk(y + k, c)

            for t in range(2):
                early(t, t % 2, 0)
            with sp.Fori(0, (TA - 4) // 2) as i:
                early(2 * i + 2, 0, i + 1)
                early(2 * i + 3, 1, i + 1)
            for t in range(TA - 2, TA):
                early(t, t % 2, t // 2)
            store_acc(TA - 1, 1)

            def routed(j, k):
                if isinstance(j, int) and j == NJ - 2:
                    load_xt(TA, 0, True)
                    load_xt(TA + 1, 1, True)
                    load_acc(TA, 0)
                sp.wait_ge(y_ready, j + 1)
                sp.dma_start(io["y_rows"](j), y_out[:, k, :]).then_inc(y_store[k], 16)

            pairs(sp, NJ, 2, routed)

            def late(i):
                t = 2 * i + TA
                even, odd = combined(i)
                if inside(t, True, -1):
                    load_xt(t + 1, 1, True)
                    for m, k, _ in combined(i - 1)[1]:
                        store_out(m, k)
                load_row(*odd[0][:2])
                if inside(t, True, -1):
                    store_acc(t - 1, 1)
                load_acc(t + 1, 1)
                load_row(*odd[1][:2])
                if inside(t, True, 2):
                    load_xt(t + 2, 0, True)
                for m, k, _ in even:
                    store_out(m, k)
                if inside(t, True, 2):
                    store_acc(t, 0)
                    load_acc(t + 2, 0)
                    for m, k, _ in combined(i + 1)[0]:
                        load_row(m, k)

            late_pairs(sp, late)
            for m in range(3 * (NT - TA) // 2 - 2, NT):
                store_out(m, m % 3)
            for k in range(3):
                sp.wait_ge(out_store[k], 16 * len(range(k, NT, 3)))

        @block.scalar
        def _(act):
            def exponentials():
                act.wait_ge(exp_in, 1)
                act.activation(work, work, ACT.Exp).then_inc(exp_out, 1)
                act.wait_ge(exp_in, 2)
                act.activation(small[:, 3, :], small[:, 3, :], ACT.Exp).then_inc(exp_out, 1)

            def silu_of(u, k):
                act.wait_ge(gu_made, u + 1)
                wait(act, h_ready, u - 1)
                act.activation(silu[:, k, :], gu_ps[:, k, 0, 0:INT], ACT.Silu).then_inc(silu_ready, 1)

            def ht_high_of(u, k):
                act.wait_ge(ht_made, u + 1)
                wait(act, down_made, u - 1)
                act.activation(ht[:, k, 0, :], h_ps[:, 0:IP], ACT.Copy).then_inc(ht_high, 1)

            def chunks(y, lo, hi):
                for c in range(lo, hi):
                    buf, _, high, _ = chunk(y, c)
                    act.wait_ge(chunk_loaded[c % 3], 16 * (USES[c % 3] * y + c // 3 + 1))
                    act.activation(high, buf, ACT.Copy).then_inc(chunk_high, 1)

            def xe_high_of(j, k):
                act.wait_ge(xe_made, j + 1)
                act.wait_ge(gu_made, UA + j - 1)
                act.activation(xt[:, k, 0, :], x_ps[:, :], ACT.Copy).then_inc(xe_high, 1)

            def y_of(j, k):
                act.wait_ge(down_made, UA + j + 1)
                wait(act, y_store[k], (j - k) * 8)
                act.activation(y_out[:, k, :], y_ps[:, k, :], ACT.Copy).then_inc(y_ready, 1)

            def shared(t, k, late, y=None):
                u, (one, two) = unit_of(t, late), buffers_of(late)
                last = not late and isinstance(t, int) and t == TA - 1

                def cut(place):
                    if y is not None:
                        chunks(y, *CUTS[k][place])

                silu_of(u + 1, two)
                cut(0)
                ht_high_of(u, one)
                if last:
                    xe_high_of(0, 0)
                cut(1)
                if inside(t, late, 1):
                    silu_of(u + 2, one)
                cut(2)
                ht_high_of(u + 1, two)
                if last:
                    xe_high_of(1, 1)
                cut(3)

            exponentials()
            silu_of(0, 0)
            for t in range(2):
                shared(t, t % 2, False, 0)
            whole, n = EXW - 2 * DIM, (TA - 4) // 2
            piece = whole // n
            for x in range(EF):
                act.dma_start(ex[0:PAD, x, whole:EXW], io["first"][x, 0:PAD, whole:EXW]).then_inc(first_loaded, 16)
            with act.Fori(0, n) as i:
                for x in range(EF):
                    act.dma_start(ex[:, x, bass.ds(i * piece, piece)],
                                  io["first"][x, :, bass.ds(i * piece, piece)]).then_inc(first_loaded, 16)
                    shared(2 * i + 2 + x, x, False, i + 1)
            for t in range(TA - 2, TA):
                shared(t, t % 2, False, t // 2)
            act.wait_ge(chunk_low, NC * (E - EF))
            silu_of(UA, 0)

            def routed(j, k):
                if is_between(j, 0, NJ - 1):
                    silu_of(UA + j + 1, 1 - k)
                ht_high_of(UA + j, k)
                if is_between(j, 0, NJ - 2):
                    xe_high_of(j + 2, k)
                if is_between(j, 1, NJ):
                    y_of(j - 1, 1 - k)

            pairs(act, NJ, 4, routed)
            y_of(NJ - 1, (NJ - 1) % 2)
            silu_of(unit_of(TA, True), buffers_of(True)[0])
            shared_steps(act, True, lambda t, k: shared(t, k, True))

        @block.vector
        def _(dve):
            links = [0]

            def link(ins):
                links[0] += 1
                ins.then_inc(chain, 1)
                dve.wait_ge(chain, links[0])

            dve.memset(h[:, :, INT:IP], 0.0).then_inc(h_pad, 1)
            iota_e = iota[:, 0:E].unsqueeze(1).to_broadcast([P, NT, E])

            def spread(v):
                return v.unsqueeze(2).to_broadcast([P, NT, E])

            def best(scores, peak, top, pick):
                link(dve.tensor_reduce(peak, scores, AX.X, ALU.max))
                link(dve.tensor_tensor(top, scores, spread(peak), ALU.is_ge))
                link(dve.scalar_tensor_tensor(out=top, in0=top, scalar=-float(E), in1=iota_e, op0=ALU.mult, op1=ALU.add))
                link(dve.tensor_reduce(pick, top, AX.X, ALU.min))
                link(dve.tensor_tensor(top, top, spread(pick), ALU.is_equal))

            peak1, peak2, pick, e2, total, p1, p2, den = (small[:, i, :] for i in range(8))
            padded, upto, base = (tiles[:, i, :] for i in range(1, 4))

            def first_expert():
                best(logits[:, :, :], peak1, top1[:, :, :], pick)
                link(dve.scalar_tensor_tensor(out=work, in0=top1[:, :, :], scalar=-3e38, in1=logits[:, :, :],
                                              op0=ALU.mult, op1=ALU.add))

            def second_expert():
                best(work, peak2, top2[:, :, :], pick)
                dve.tensor_tensor(rank[:, 0, :, :], top1[:, :, :], top2[:, :, :], ALU.add).then_inc(top_ready, 1)

            def differences():
                dve.tensor_tensor(work, logits[:, :, :], spread(peak1), ALU.subtract).then_inc(exp_in, 1)
                dve.tensor_tensor(e2, peak2, peak1, ALU.subtract).then_inc(exp_in, 1)

            def weights():
                dve.wait_ge(exp_out, 2)
                link(dve.tensor_reduce(total, work, AX.X, ALU.add))
                link(dve.reciprocal(p1, total))
                link(dve.tensor_tensor(p2, e2, p1, ALU.mult))
                link(dve.scalar_tensor_tensor(out=den, in0=p1, scalar=1e-20, in1=p2, op0=ALU.add, op1=ALU.add))
                link(dve.reciprocal(den, den))
                link(dve.tensor_scalar(den, den, gates[:, 3:4], None, ALU.mult))
                link(dve.tensor_tensor(weight[:, 0, :], p1, den, ALU.mult))
                link(dve.tensor_tensor(weight[:, 1, :], p2, den, ALU.mult))

            def starts():
                dve.wait_ge(rank_made, 1)
                link(dve.tensor_copy(rank, x_ps[:, :].rearrange("p (a t e) -> p a t e", a=2, e=E)))
                for x in range(E):
                    ins = dve.tensor_tensor_scan(before[:, :, x], ones[:, 0:NT], rank[:, 1, :, x], 0.0, ALU.mult, ALU.add)
                link(ins)
                link(dve.tensor_scalar(tiles_i[:, 0, :], before[:, NT - 1, :], float(P - 1), None, ALU.add))
                link(dve.tensor_scalar(tiles_i[:, 1, :], tiles_i[:, 0, :], 7, None, ALU.logical_shift_right))
                link(dve.tensor_copy(padded, tiles_i[:, 1, :]))
                link(dve.tensor_tensor_scan(upto, ones[:, 0:E], padded, 0.0, ALU.mult, ALU.add))
                link(dve.tensor_tensor(base, upto, padded, ALU.subtract))
                link(dve.tensor_scalar(base, base, float(P), None, ALU.mult))

            def slots():
                link(dve.tensor_tensor(before, before, rank[:, 1, :, :], ALU.subtract))
                link(dve.tensor_tensor(before, before, rank[:, 0, :, :], ALU.add))
                link(dve.tensor_tensor(before, before, base.unsqueeze(1).to_broadcast([P, NT, E]), ALU.add))
                for r, top in enumerate((top1, top2)):
                    link(dve.tensor_tensor(work, before, top[:, :, :], ALU.mult))
                    link(dve.tensor_reduce(slot_f[:, 0, r, :], work, AX.X, ALU.add))

            def table_places():
                link(dve.tensor_copy(slot[:, :, :], slot_f[:, 0, :, :]))
                link(dve.tensor_scalar(slot_part[:, 0, :, :], slot[:, :, :], P - 1, None, ALU.bitwise_and))
                link(dve.tensor_scalar(slot_part[:, 1, :, :], slot[:, :, :], 7, None, ALU.logical_shift_right))
                link(dve.tensor_copy(slot_f[:, :, :, :], slot_part[:, :, :, :]))
                dve.scalar_tensor_tensor(out=table_at[:, :, :], in0=slot_f[:, 0, :, :], scalar=float(NJ),
                                         in1=slot_f[:, 1, :, :], op0=ALU.mult, op1=ALU.add).then_inc(slots_ready, 1)

            def tile_experts():
                link(dve.tensor_scalar(experts_f[:, :], iota[0:1, E:E + NJ], tiles[0:1, 2, 0:1], None, ALU.is_ge))
                for x in range(1, E):
                    link(dve.scalar_tensor_tensor(out=experts_f[:, :], in0=iota[0:1, E:E + NJ], scalar=tiles[0:1, 2, x:x + 1],
                                                  in1=experts_f[:, :], op0=ALU.is_ge, op1=ALU.add))
                dve.tensor_scalar(experts[:, :], experts_f[:, :], float(E - 1), None, ALU.min).then_inc(experts_ready, 1)

            routing = {(0, 1): weights, (0, 2): starts, (1, 2): slots, (2, 0): table_places, (2, 2): tile_experts}

            def h_of(u, k):
                dve.wait_ge(silu_ready, u + 1)
                wait(dve, ht_made, u - 1)
                dve.tensor_tensor(h[:, k, 0:INT], silu[:, k, :], gu_ps[:, k, 1, 0:INT], ALU.mult).then_inc(h_ready, 1)

            def ht_low_of(u, k):
                dve.wait_ge(ht_high, u + 1)
                dve.tensor_tensor(ht[:, k, 1, :], h_ps[:, 0:IP], ht[:, k, 0, :], ALU.subtract).then_inc(ht_low, 1)

            def acc_of(t, k, late):
                dve.wait_ge(down_made, unit_of(t, late) + 2)
                dve.wait_ge(acc_loaded[k], (t - k) * 8 + 16)
                dve.scalar_tensor_tensor(out=acc[:, k, :], in0=y_ps[:, k, :], scalar=gates[:, 3:4], in1=acc[:, k, :],
                                         op0=ALU.mult, op1=ALU.add).then_inc(acc_ready, 1)

            def chunks(y, lo, hi):
                for c in range(lo, hi):
                    buf, _, high, low = chunk(y, c)
                    dve.wait_ge(chunk_high, NC * y + c + 1)
                    dve.tensor_tensor(low, buf, high, ALU.subtract).then_inc(chunk_low, 1)

            def xe_low_of(j, k):
                dve.wait_ge(xe_high, j + 1)
                dve.tensor_tensor(xt[:, k, 1, :], x_ps[:, :], xt[:, k, 0, :], ALU.subtract).then_inc(xe_low, 1)

            def shared(t, k, late, y=None, row=None):
                u, (one, two) = unit_of(t, late), buffers_of(late)
                last = not late and isinstance(t, int) and t == TA - 1

                def between(place):
                    if y is not None:
                        chunks(y, *CUTS[k][place])
                    if not late and isinstance(t, int) and (t, place) in routing:
                        routing[t, place]()

                h_of(u + 1, two)
                between(0)
                ht_low_of(u, one)
                if last:
                    xe_low_of(0, 0)
                between(1)
                if inside(t, late, -1):
                    acc_of(t - 1, 1 - k, late)
                if inside(t, late, 1):
                    h_of(u + 2, one)
                between(2)
                if row is not None:
                    combine(*row)
                ht_low_of(u + 1, two)
                if last:
                    xe_low_of(1, 1)
                between(3)

            first_expert()
            second_expert()
            differences()
            h_of(0, 0)
            for t in range(4):
                shared(t, t % 2, False, t // 2)
            with dve.Fori(0, (TA - 6) // 2) as i:
                shared(2 * i + 4, 0, False, i + 2)
                shared(2 * i + 5, 1, False, i + 2)
            for t in range(TA - 2, TA):
                shared(t, t % 2, False, t // 2)
            acc_of(TA - 1, 1, False)
            h_of(UA, 0)

            def routed(j, k):
                if is_between(j, 0, NJ - 1):
                    h_of(UA + j + 1, 1 - k)
                ht_low_of(UA + j, k)
                if is_between(j, 0, NJ - 2):
                    xe_low_of(j + 2, k)

            def column(m):
                return slice(m, m + 1) if isinstance(m, int) else bass.ds(m, 1)

            def combine(m, k, turn, row=None):
                dve.wait_ge(y_loaded[k], turn * 32 + 32)
                if row is None:
                    row = row_in[:, k, :]
                    dve.wait_ge(row_loaded[k], turn * 16 + 16)
                else:
                    dve.wait_ge(acc_ready, m + 1)
                dve.scalar_tensor_tensor(out=row, in0=y_in[:, k, 0, :], scalar=weight[:, 0, column(m)], in1=row,
                                         op0=ALU.mult, op1=ALU.add).then_inc(chain, 1)
                dve.wait_ge(chain, links[0] + m + 1)
                wait(dve, out_store[k], turn * 16)
                dve.scalar_tensor_tensor(out=out_row[:, k, :], in0=y_in[:, k, 1, :], scalar=weight[:, 1, column(m)],
                                         in1=row, op0=ALU.mult, op1=ALU.add).then_inc(row_ready, 1)

            def late(i):
                for k, rows_now in enumerate(combined(i)):
                    shared(2 * i + TA + k, k, True, row=rows_now[0] if len(rows_now) == 2 else None)
                    for row in rows_now[-1:]:
                        combine(*row)

            pairs(dve, NJ, 2, routed)
            h_of(unit_of(TA, True), buffers_of(True)[0])
            late_pairs(dve, late)
            combine(NT - 2, (NT - 2) % 3, (NT - 2) // 3, acc[:, 0, :])
            acc_of(NT - 1, 1, True)
            combine(NT - 1, (NT - 1) % 3, (NT - 1) // 3, acc[:, 1, :])

        @block.gpsimd
        def _(pool):
            links = [0]

            def link(ins):
                links[0] += 1
                ins.then_inc(pool_zero, 1)
                pool.wait_ge(pool_zero, links[0])

            link(pool.memset(slot_token[:, :], 0))
            pool.dma_start(io["table"], slot_token[:, :]).then_inc(table_clear, 16)
            for s in keep["x1_store"] + keep["xn_store"] + keep["xt_store"]:
                pool.wait_ge(s, 16 * B)
            link(pool.memset(ex[PAD:P, :, EXW - 2 * DIM:EXW], 0.0))
            pool.wait_ge(table_clear, 16)
            pool.wait_ge(slots_ready, 1)

            def put(i, k):
                wait(pool, put_done[k], 64 * ((i - k) // 2) if isinstance(i, int) else (i - k) * 32)
                two_tiles = slice(2 * i, 2 * i + 2) if isinstance(i, int) else bass.ds(2 * i, 2)
                pool.tensor_copy(put_at[:, k, :, :], table_at[:, :, two_tiles]).then_inc(staged, 1)
                pool.tensor_copy(put_token[:, k, :], token[:, two_tiles]).then_inc(staged, 1)
                wait_alone(pool, staged, 2 * i + 2, passed)
                for r in range(2):
                    for q in range(2):
                        pool.indirect_dma_start(io["table_cells"], bass.IndirectOffsetOnAxis(ap=put_at[:, k, r, q:q + 1], axis=0),
                                                put_token[:, k, q:q + 1], None).then_inc(put_done[k], 16)

            pairs(pool, NT // 2, 2, put)

            def fetch(j, k):
                wait(pool, xe_made, j - 1)
                pool.tensor_copy(get_at[:, k, 0:1], slot_token[:, j:j + 1] if isinstance(j, int)
                                 else slot_token[:, bass.ds(j, 1)]).then_inc(staged, 1)
                wait_alone(pool, staged, NT + j + 1, passed)
                pool.indirect_dma_start(xg[:, k, :], None, io["xn_rows"],
                                        bass.IndirectOffsetOnAxis(ap=get_at[:, k, 0:1], axis=0)).then_inc(xg_loaded[k], 16)

            for k in range(2):
                pool.wait_ge(put_done[k], 64 * (NT // 4))
            pool.dma_start(slot_token[:, :], io["table"]).then_inc(table_loaded, 16)
            pool.wait_ge(table_loaded, 16)
            pairs(pool, NJ, 2, fetch)
            for k in range(2):
                pool.wait_ge(y_store[k], 16 * len(range(k, NJ, 2)))

            def collect(m, k):
                wait(pool, row_ready, m - 2)
                pool.tensor_copy(get_at[:, k, :], slot[:, :, m] if isinstance(m, int)
                                 else slot[:, :, bass.ds(m, 1)].rearrange("p r a -> p (r a)")).then_inc(staged, 1)
                wait_alone(pool, staged, NT + NJ + m + 1, passed)
                for r in range(2):
                    pool.indirect_dma_start(y_in[:, k, r, :], None, io["y_all"],
                                            bass.IndirectOffsetOnAxis(ap=get_at[:, k, r:r + 1], axis=0)).then_inc(y_loaded[k], 16)

            for m in range(3):
                collect(m, m)
            with pool.Fori(0, NT // 3 - 1) as i:
                for k in range(3):
                    collect(3 * i + 3 + k, k)
            for m in range(NT // 3 * 3, NT):
                collect(m, m % 3)

        @block.tensor
        def _(pe):
            PARTS = ((0, 0), (0, 1), (1, 0))

            def up(u, k, slot_k, wu):
                wait(pe, h_ready, u - 1)
                for c in range(KC):
                    for n, (a, w) in enumerate(PARTS):
                        for side in range(2):
                            mm = pe.matmul(gu_ps[:, k, side, 0:INT], xt[:, slot_k, a, c * P:(c + 1) * P], wu(w, c, side),
                                           start=(c == 0 and n == 0), stop=(c == KC - 1 and n == 2))
                mm.then_inc(gu_made, 1)

            def turn_h(u, k):
                pe.wait_ge(h_ready, u + 1)
                wait(pe, ht_low, u)
                for c in range(IC):
                    mm = pe.transpose(h_ps[:, c * P:(c + 1) * P], h[:, k, c * P:(c + 1) * P], ident[:, :])
                mm.then_inc(ht_made, 1)

            def down(u, k, yk, wd, start, stop):
                pe.wait_ge(ht_high, u + 1)
                pe.wait_ge(ht_low, u + 1)
                for c in range(IC):
                    for n, (a, w) in enumerate(PARTS):
                        mm = pe.matmul(y_ps[:, yk, :], ht[:, k, a, c * P:(c + 1) * P], wd(w, c),
                                       start=(start and c == 0 and n == 0), stop=(stop and c == IC - 1 and n == 2))
                mm.then_inc(down_made, 1)

            def up_shared(i):
                return lambda w, c, side: shu[w][:, i, c, side * INT:(side + 1) * INT]

            def down_shared(i):
                return lambda w, c: shd[w][:, i, c, :]

            def turn_x(j, k):
                pe.wait_ge(xg_loaded[k], (j - k) * 8 + 16)
                wait(pe, xe_low, j)
                for c in range(KC):
                    mm = pe.transpose(x_ps[:, c * P:(c + 1) * P], xg[:, k, c * P:(c + 1) * P], ident[:, :])
                mm.then_inc(xe_made, 1)

            def shared(t, k, late):
                u, (one, two) = unit_of(t, late), buffers_of(late)
                last = not late and isinstance(t, int) and t == TA - 1
                up(u + 1, two, k, up_shared(1))
                turn_h(u, one)
                if last:
                    turn_x(0, 0)
                if inside(t, late, -1):
                    down(u - 1, two, 1 - k, down_shared(1), False, True)
                if inside(t, late, 1):
                    pe.wait_ge(xt_loaded[1 - k], (t + 1 - (1 - k)) * 8 + 16)
                    up(u + 2, one, 1 - k, up_shared(0))
                turn_h(u + 1, two)
                if last:
                    turn_x(1, 1)
                if late and isinstance(t, int) and t < TA + 2:
                    pe.wait_ge(y_ready, NJ)
                else:
                    wait(pe, acc_ready, t - 1)
                down(u, one, k, down_shared(0), True, False)

            def rank_in_tile():
                pe.wait_ge(top_ready, 1)
                chosen = rank[:, 0, :, :].rearrange("p t e -> p (t e)")
                pe.matmul(x_ps[:, 0:NT * E], tri[:, :], chosen, start=True, stop=True)
                pe.matmul(x_ps[:, NT * E:2 * NT * E], ones[:, :], chosen, start=True, stop=True).then_inc(rank_made, 1)

            pe.wait_ge(h_pad, 1)
            pe.wait_ge(xt_loaded[0], 16)
            up(0, 0, 0, up_shared(0))
            rank_in_tile()
            shared_steps(pe, False, lambda t, k: shared(t, k, False))
            down(UA - 1, 1, 1, down_shared(1), False, True)

            def expert(j):
                at = slice(j, j + 1) if isinstance(j, int) else bass.ds(j, 1)
                return pe.value_load(experts[0:1, at], min_val=0, max_val=E - 1)

            def gu_of(r, w, c, side):
                at = part_start(w, c) + side * INT
                return ex[:, bass.ds(r, 1), at:at + INT].rearrange("p a n -> p (a n)")

            def down_of(r, w, c):
                at = part_start(w, KC + c)
                return ex[:, bass.ds(r, 1), at:at + DIM].rearrange("p a n -> p (a n)")

            def up_routed(j, k):
                r = expert(j)
                pe.wait_ge(xe_low, j + 1)
                up(UA + j, k, k, lambda w, c, side: gu_of(r, w, c, side))

            def down_routed(j, k):
                r = expert(j)
                if isinstance(j, int) and j < 2:
                    pe.wait_ge(acc_ready, TA)
                else:
                    pe.wait_ge(y_ready, j - 1)
                down(UA + j, k, k, lambda w, c: down_of(r, w, c), True, True)

            pe.wait_ge(experts_ready, 1)
            pe.wait_ge(pool_zero, 2)
            pe.wait_ge(first_loaded, 16 * EF * (1 + (TA - 4) // 2))
            pe.wait_ge(chunk_low, NC * (E - EF))
            up_routed(0, 0)

            def routed(j, k):
                if is_between(j, 0, NJ - 1):
                    up_routed(j + 1, 1 - k)
                turn_h(UA + j, k)
                if is_between(j, 0, NJ - 2):
                    turn_x(j + 2, k)
                if is_between(j, 1, NJ):
                    down_routed(j - 1, 1 - k)

            pairs(pe, NJ, 4, routed)
            down_routed(NJ - 1, (NJ - 1) % 2)
            pe.wait_ge(xt_loaded[0], 16 * (TA // 2 + 1))
            up(unit_of(TA, True), buffers_of(True)[0], 0, up_shared(0))
            shared_steps(pe, True, lambda t, k: shared(t, k, True))
            down(unit_of(NT, True) - 1, buffers_of(True)[1], 1, down_shared(1), False, True)


def build(nc, a, out):
    x_tiles = a["x"].rearrange("b (q p) c -> p b q c", p=P)
    scratch = {n: nc.dram_tensor(n, shape, dt).ap() for n, shape, dt in (
        ("gate_s", (P, B, 2, DIM), F32), ("x1_s", (NT, P, DIM), F32), ("xn_s", (NT * P, DIM), F32),
        ("xt_s", (NT, P, 2, DIM), BF16), ("acc_s", (NT, P, DIM), F32), ("y_s", (NJ * P, DIM), F32),
        ("table_s", (P * NJ, 1), I32), ("first_s", (EF, P, EXW), BF16))}
    out_tiles = out.rearrange("b (q p) c -> (b q) p c", p=P)
    ctx_rows = a["ctx"].rearrange("b (q p) c -> p b q c", p=P)

    def pick(ap, i, how):
        if isinstance(i, int):
            return ap[i]
        return ap[bass.ds(i, 1)].rearrange(how)

    def batch(ap, b):
        if isinstance(b, int):
            return ap[:, b, :, :]
        return ap[:, bass.ds(b, 1), :, :].rearrange("p a q c -> p (a q) c")

    def first_parts(x, c):
        rows, width = chunk_shape(c)
        start, step = part_start(0, c), part_start(1, c) - part_start(0, c)
        return scratch["first_s"][x, 0:rows, start:start + 2 * step].rearrange("r (p n) -> r p n", p=2)[:, :, 0:width]

    ctx_t = a["ctx_t"].rearrange("b h d s -> d b h s")
    io = {
        "wht": a["wht"], "ident": a["ident"], "gates": a["gates"], "wg": a["wg"], "decay": a["decay"],
        "wh": a["wh"], "wo": a["wo"], "wr": a["wr"], "affine": a["affine"], "tri": a["tri"], "ones": a["ones"],
        "iota": a["iota"], "token": a["token"], "gu": a["gu"], "down": a["down"],
        "x_batch": lambda b: batch(x_tiles, b),
        "c_batch": lambda b: batch(ctx_rows, b),
        "ct_batch": lambda b: batch(ctx_t, b),
        "gate_tile": lambda b, q: scratch["gate_s"][:, b, q, :] if isinstance(b, int)
        else scratch["gate_s"][:, bass.ds(b, 1), q, :].rearrange("p a c -> p (a c)"),
        "gate_batch": lambda b: batch(scratch["gate_s"], b),
        "x1_tile": lambda b, q: pick(scratch["x1_s"], 2 * b + q, "a p c -> (a p) c"),
        "xn_tile": lambda b, q: pick(scratch["xn_s"].rearrange("(t p) c -> t p c", p=P), 2 * b + q, "a p c -> (a p) c"),
        "xt_tile": lambda b, q: pick(scratch["xt_s"], 2 * b + q, "a p r c -> (a p) r c"),
        "xt_row": lambda t: pick(scratch["xt_s"], t, "a p r c -> (a p) r c"),
        "x1_row": lambda t: pick(scratch["x1_s"], t, "a p c -> (a p) c"),
        "acc_row": lambda t: pick(scratch["acc_s"], t, "a p c -> (a p) c"),
        "out_row": lambda t: pick(out_tiles, t, "a p c -> (a p) c"),
        "y_rows": lambda j: pick(scratch["y_s"].rearrange("(j p) c -> j p c", p=P), j, "a p c -> (a p) c"),
        "y_all": scratch["y_s"], "xn_rows": scratch["xn_s"],
        "table": scratch["table_s"].rearrange("(p j) o -> p (j o)", p=P), "table_cells": scratch["table_s"],
        "first_parts": first_parts,
        "first": scratch["first_s"],
        "gu_chunk": lambda x, c: pick(a["gu"], x, "a p c n -> (a p) c n")[:, c, :],
        "down_chunk": lambda x, i, n: pick(a["down"], x, "a i c -> (a i) c")[i * P:i * P + n, :],
    }
    with ExitStack() as ctx:
        def sb(name, shape, dt):
            return ctx.enter_context(nc.sbuf_tensor(name, shape, dt))

        keep = {
            "ident": sb("ident", [P, P], F32), "gates": sb("gates", [P, 4], F32), "logits": sb("logits", [P, NT, E], F32),
            "shu_hi": sb("shu_hi", [P, 2, KC, 2 * INT], BF16), "shu_lo": sb("shu_lo", [P, 2, KC, 2 * INT], BF16),
            "shd_hi": sb("shd_hi", [P, 2, IC, DIM], BF16), "shd_lo": sb("shd_lo", [P, 2, IC, DIM], BF16),
            "xt_parts": sb("xt_parts", [P, 2, 2, DIM], BF16), "tri": sb("tri", [P, P], F32), "ones": sb("ones", [P, P], F32),
            "iota": sb("iota", [P, E + NJ], F32), "token": sb("token", [P, NT], I32),
            **{n: [ctx.enter_context(nc.semaphore(f"{n}{k}")) for k in range(2)]
               for n in ("gate_store", "x1_store", "xn_store", "xt_store", "xt_loaded")}}
        with ExitStack() as two:
            keep["w_out"] = two.enter_context(nc.sbuf_tensor("w_out", [P, 2, DIM], F32))
            for n, dt in (("c_in", F32), ("c_hi", F32R), ("c_lo", F32R)):
                keep[n] = two.enter_context(nc.sbuf_tensor(n, [P, 2, 2, DIM], dt))
            for n, dt in (("wh", F32), ("wh_hi", F32R), ("wh_lo", F32R)):
                keep[n] = two.enter_context(nc.sbuf_tensor(n, [P, H, HD], dt))
            for n in ("at_hi", "at_lo"):
                keep[n] = two.enter_context(nc.sbuf_tensor(n, [P, H, 2, S], F32R))
            scores_stage(nc, io, keep)
            mix_stage(nc, io, keep)
        ffn_stage(nc, io, keep)


def shape_constants():
    gam = (1.0 - 2.0 ** (-5.0 - np.arange(H, dtype=np.float32))).astype(np.float32)
    idx = np.arange(S, dtype=np.float32)
    expo = idx[None, :] - idx[:, None]
    d = np.where(expo[None] <= 0, gam[:, None, None] ** expo[None], 0.0).astype(np.float32)
    d = d / np.sqrt(d.sum(axis=-1))[:, None, :] / np.float32(np.sqrt(HD))
    dt = d.transpose(2, 0, 1)
    decay = np.concatenate([dt[0:P, 0:2].reshape(P, -1), dt[0:P, 2:4].reshape(P, -1), dt[P:S, :, P:S].reshape(P, -1)], 1)
    iota = np.concatenate([np.arange(E), np.arange(NJ)])
    return {
        "ident": np.eye(P, dtype=np.float32), "tri": np.triu(np.ones((P, P), np.float32), 1),
        "ones": np.ones((P, P), np.float32), "decay": decay.reshape(P, 3, DIM).astype(np.float32),
        "iota": np.broadcast_to(iota.astype(np.float32), (P, E + NJ)),
        "token": (np.arange(NT)[None, :] * P + np.arange(P)[:, None]).astype(np.int32)}


def kernel(x, ctx_2048, g_xattn, g_ffn, L0_xattn_Wh, L0_xattn_wg_w, L0_xattn_wo_w, L0_xattn_gn_gamma,
           L0_xattn_gn_beta, L0_ffn_gate_w, L0_ffn_expert_gate, L0_ffn_expert_up, L0_ffn_expert_down,
           L0_ffn_shared_gate, L0_ffn_shared_up, L0_ffn_shared_down):
    import concourse.bacc as bacc
    from concourse.bass_utils import run_bass_kernel_spmd

    def rows(w, n=DIM):
        return np.asarray(w).reshape(-1, P, n).transpose(1, 0, 2)

    ctx = np.asarray(ctx_2048)
    wh = np.asarray(L0_xattn_Wh)
    gate = np.concatenate([np.asarray(L0_ffn_expert_gate), np.asarray(L0_ffn_shared_gate).reshape(2, INT, DIM)])
    up = np.concatenate([np.asarray(L0_ffn_expert_up), np.asarray(L0_ffn_shared_up).reshape(2, INT, DIM)])
    gu = np.concatenate([gate, up], 1).transpose(0, 2, 1).reshape(NB, KC, P, 2 * INT).transpose(0, 2, 1, 3)
    down = np.concatenate([np.asarray(L0_ffn_expert_down).transpose(0, 2, 1),
                           np.asarray(L0_ffn_shared_down).T.reshape(2, INT, DIM)])
    arrays = {
        "x": np.asarray(x), "ctx": ctx, "ctx_t": ctx.reshape(B, S, H, HD).transpose(0, 2, 3, 1),
        "gates": np.broadcast_to(np.concatenate([np.asarray(g_xattn), np.asarray(g_ffn)]), (P, 2)),
        "wht": wh.transpose(2, 0, 1), "wh": wh.transpose(1, 0, 2), "wg": rows(L0_xattn_wg_w), "wo": rows(L0_xattn_wo_w),
        "wr": rows(np.asarray(L0_ffn_gate_w).T, E),
        "affine": np.broadcast_to(np.stack([np.asarray(L0_xattn_gn_gamma), np.asarray(L0_xattn_gn_beta)]), (P, 2, DIM)),
        "gu": gu, "down": down, **shape_constants()}
    arrays = {n: np.ascontiguousarray(v) for n, v in arrays.items()}
    nc = bacc.Bacc("TRN2", target_bir_lowering=False, num_devices=1)
    aps = {n: nc.dram_tensor(n + "_dram", v.shape, mybir.dt.from_np(v.dtype), kind="ExternalInput").ap()
           for n, v in arrays.items()}
    out = nc.dram_tensor("out_dram", (B, S, DIM), F32, kind="ExternalOutput").ap()
    build(nc, aps, out)
    r = run_bass_kernel_spmd(nc, [{n + "_dram": v for n, v in arrays.items()}], core_ids=[0])
    return r.results[0]["out_dram"]
```
